# Optimizing a Trainium2 kernel written in Bass

```python
import numpy as np
import jax
import jax.numpy as jnp

def _softmax(x, axis=-1):
    return jax.nn.softmax(x, axis=axis)

def _gelu(x):
    return jax.nn.gelu(x, approximate=True)

def _silu(x):
    return jax.nn.silu(x)

def _sigmoid(x):
    return jax.nn.sigmoid(x)

def _layernorm(x, axis=-1, eps=1e-05):
    m = jnp.mean(x, axis=axis, keepdims=True)
    v = jnp.var(x, axis=axis, keepdims=True)
    return (x - m) / jnp.sqrt(v + eps)

def _scatter_add(tgt, idx, src, axis=0):
    return tgt.at[idx].add(src)

def _segment_sum(src, seg, n):
    return jax.ops.segment_sum(src, seg, n)
kernel_name = 'mk_xattn_ffn_d2_seqx_r2_1a0476'

def setup_inputs(seed: int=0):
    np.random.seed(seed)
    _w = jnp.asarray

    def _rec_inputs():
        import jax
        import jax.numpy as jnp
        _rk = jax.random.key(seed)
        x = 7.22e-05 + 1 * jax.random.normal(jax.random.fold_in(_rk, 1), (8, 100, 512), jnp.float32)
        _lenS = 100 - jax.random.randint(jax.random.fold_in(_rk, 7), (8,), 0, max(1, 100 // 4) + 1, jnp.int32)
        _lenS2 = 722 - jax.random.randint(jax.random.fold_in(_rk, 8), (8,), 0, max(1, 722 // 4) + 1, jnp.int32)
        _ctx_768P = jax.random.normal(jax.random.fold_in(_rk, 11), (8, 16, 384), jnp.float32)
        _ctx_768c = jax.random.dirichlet(jax.random.fold_in(_rk, 511), 0.3 * jnp.ones((16,), jnp.float32), (8, 722))
        _ctx_768t = jnp.einsum('bsk,bkd->bsd', _ctx_768c, _ctx_768P)
        _ctx_768t = _ctx_768t * jax.lax.rsqrt(jnp.mean(jnp.square(_ctx_768t)) + 1e-12) * 0.953939
        ctx_768 = 3.88148e-05 + 0.999967 * (_ctx_768t + 0.3 * jax.random.normal(jax.random.fold_in(_rk, 611), (8, 722, 384), jnp.float32))
        _validS = jnp.arange(100)[None, :] < _lenS[:, None]
        _validS2 = jnp.arange(722)[None, :] < _lenS2[:, None]
        _causal = jnp.tril(jnp.ones((100, 100), dtype=bool))
        mask_BxS_bf1 = jnp.ones((8, 100), dtype=bool)
        mask_BxS2_bf1 = jnp.ones((8, 722), dtype=bool)
        mask_BxS2_bk0 = jnp.logical_not(jnp.broadcast_to(_validS2[:, :], (8, 722)))
        return (x, ctx_768, mask_BxS_bf1, mask_BxS2_bf1, mask_BxS2_bk0)
    x, ctx_768, mask_BxS_bf1, mask_BxS2_bf1, mask_BxS2_bk0 = _rec_inputs()

    def _L0_xattn_setup():
        import jax, jax.numpy as jnp
        import numpy as np
        B, T, DT, G, DV = (16, 256, 512, 288, 384)
        H, DH = (4, 32)
        INNER = H * DH
        HID = 4 * DT
        N_STATE = 64
        K_TOP = 32

        def layernorm(x, g, b, eps=1e-05):
            m = x.mean(-1, keepdims=True)
            v = x.var(-1, keepdims=True)
            return (x - m) * jax.lax.rsqrt(v + eps) * g + b

        def s4d(x, log_dt, A_re, A_im, C_re, C_im, D_skip):
            Bb, L, D = x.shape
            dt = jnp.exp(log_dt)
            A = A_re + 1j * A_im
            C = C_re + 1j * C_im
            dtA = dt[:, None] * A
            dC = C * (jnp.exp(dtA) - 1.0) / A
            powers = jnp.exp(dtA[:, :, None] * jnp.arange(L))
            K = 2.0 * jnp.einsum('dn,dnl->dl', dC, powers).real
            n = 2 * L
            Kf = jnp.fft.rfft(K, n=n, axis=-1)
            xf = jnp.fft.rfft(x, n=n, axis=1)
            y = jnp.fft.irfft(xf * Kf.T[None], n=n, axis=1)[:, :L]
            return y + x * D_skip
        key = jax.random.key(seed)
        ks = jax.random.split(key, 16)
        s = 0.02
        inp = {'x_text': jax.random.normal(ks[0], (B, T, DT), jnp.float32), 'x_vision': jax.random.normal(ks[1], (B, G, DV), jnp.float32), 'text_mask': jnp.ones((B, T), bool), 'vision_mask': jnp.ones((B, G), bool), 'Wq': jax.random.normal(ks[2], (DT, INNER), jnp.float32) * s, 'Wk': jax.random.normal(ks[3], (DV, INNER), jnp.float32) * s, 'Wv': jax.random.normal(ks[4], (DV, DT), jnp.float32) * s, 'W_film_in': jax.random.normal(ks[5], (DT, 2 * DT), jnp.float32) * s, 'b_film_in': jnp.zeros((2 * DT,), jnp.float32), 'W_film_out': jax.random.normal(ks[6], (DT, 2 * DT), jnp.float32) * s, 'b_film_out': jnp.zeros((2 * DT,), jnp.float32), 'g_norm_in': jnp.ones((DT,), jnp.float32), 'b_norm_in': jnp.zeros((DT,), jnp.float32), 'g_norm_out': jnp.ones((DT,), jnp.float32), 'b_norm_out': jnp.zeros((DT,), jnp.float32), 'g_ffn': jnp.ones((DT,), jnp.float32), 'b_ffn': jnp.zeros((DT,), jnp.float32), 'W1': jax.random.normal(ks[7], (DT, HID), jnp.float32) * s, 'b1': jnp.zeros((HID,), jnp.float32), 'W2': jax.random.normal(ks[8], (HID, DT), jnp.float32) * s, 'b2': jnp.zeros((DT,), jnp.float32), 'log_dt': jnp.log(0.001) + jax.random.uniform(ks[9], (DT,), jnp.float32) * (jnp.log(0.1) - jnp.log(0.001)), 'A_re': -0.5 * jnp.ones((DT, N_STATE), jnp.float32), 'A_im': jnp.tile(jnp.pi * jnp.arange(N_STATE, dtype=jnp.float32), (DT, 1)), 'C_re': jax.random.normal(ks[10], (DT, N_STATE), jnp.float32) * 0.5 ** 0.5, 'C_im': jax.random.normal(ks[11], (DT, N_STATE), jnp.float32) * 0.5 ** 0.5, 'D_skip': jax.random.normal(ks[12], (DT,), jnp.float32), 'mod_gate': jnp.array(0.5, jnp.float32)}
        return inp
    _L0_xattn_all = _L0_xattn_setup()
    _L0_xattn_in = {k: v for k, v in _L0_xattn_all.items() if k in ('Wq', 'Wk', 'Wv', 'W_film_in', 'b_film_in', 'W_film_out', 'b_film_out', 'g_norm_in', 'b_norm_in', 'g_norm_out', 'b_norm_out', 'g_ffn', 'b_ffn', 'W1', 'b1', 'W2', 'b2', 'log_dt', 'A_re', 'A_im', 'C_re', 'C_im', 'D_skip', 'mod_gate')}
    del _L0_xattn_all

    def _L0_ffn_setup():
        import math
        import jax, jax.numpy as jnp
        import numpy as np
        B, L, D, F_FF, E = (4, 1024, 512, 2048, 8)
        TOP_K = 1
        CAPACITY_FACTOR = 1.25
        key = jax.random.key(seed)
        ks = jax.random.split(key, 4)
        h = jax.random.normal(ks[0], (B, L, D), dtype=jnp.float32)
        gate_w = jax.random.normal(ks[1], (E, D), dtype=jnp.float32) * 0.02
        gate_b = jnp.zeros((E,), dtype=jnp.float32)
        w1 = jax.random.normal(ks[2], (E, D, F_FF), dtype=jnp.float32) * 0.02
        b1 = jnp.zeros((E, F_FF), dtype=jnp.float32)
        w2 = jax.random.normal(ks[3], (E, F_FF, D), dtype=jnp.float32) * 0.02
        b2 = jnp.zeros((E, D), dtype=jnp.float32)
        return {'h': h, 'gate_w': gate_w, 'gate_b': gate_b, 'w1': w1, 'b1': b1, 'w2': w2, 'b2': b2}
    _L0_ffn_all = _L0_ffn_setup()
    _L0_ffn_in = {k: v for k, v in _L0_ffn_all.items() if k in ('gate_w', 'gate_b', 'w1', 'b1', 'w2', 'b2')}
    del _L0_ffn_all

    def _L1_xattn_setup():
        import jax, jax.numpy as jnp
        import numpy as np
        DIM_IN, DIM_LAT, DIM_HEAD = (384, 512, 64)
        INNER = max(DIM_LAT, DIM_IN)
        HEADS = INNER // DIM_HEAD
        SCALE = DIM_HEAD ** (-0.5)
        RMS_EPS = 1e-08
        LN_EPS = 1e-05

        def layernorm(x, g, b):
            mu = jnp.mean(x, axis=-1, keepdims=True)
            var = jnp.mean((x - mu) ** 2, axis=-1, keepdims=True)
            return (x - mu) * jax.lax.rsqrt(var + LN_EPS) * g + b

        def rmsnorm(x, gamma):
            norm = jnp.sqrt(jnp.sum(x * x, axis=-1, keepdims=True)) * x.shape[-1] ** (-0.5)
            return x / jnp.maximum(norm, RMS_EPS) * gamma
        key = jax.random.key(seed)
        ks = jax.random.split(key, 12)
        b, n, m = (4, 2048, 256)
        x = jax.random.normal(ks[0], (b, n, DIM_IN), jnp.float32)
        latents = jax.random.normal(ks[1], (b, m, DIM_LAT), jnp.float32)
        mask = jax.random.randint(ks[2], (b, n), 0, 2).astype(bool)
        s = lambda k, sh, fan: jax.random.normal(k, sh, jnp.float32) * fan ** (-0.5)
        return {'x': x, 'latents': latents, 'mask': mask, 'ln_x_g': jnp.ones((DIM_IN,), jnp.float32), 'ln_x_b': jnp.zeros((DIM_IN,), jnp.float32), 'ln_l_g': jnp.ones((DIM_LAT,), jnp.float32), 'ln_l_b': jnp.zeros((DIM_LAT,), jnp.float32), 'qn_g': jnp.ones((DIM_HEAD,), jnp.float32), 'kn_g': jnp.ones((DIM_HEAD,), jnp.float32), 'Wq': s(ks[3], (INNER, DIM_LAT), DIM_LAT), 'Wkv': s(ks[4], (2 * INNER, DIM_IN), DIM_IN), 'Wlkv': s(ks[5], (2 * INNER, DIM_LAT), DIM_LAT), 'Wo': s(ks[6], (DIM_LAT, INNER), INNER), 'bo': jnp.zeros((DIM_LAT,), jnp.float32)}
    _L1_xattn_all = _L1_xattn_setup()
    _L1_xattn_in = {k: v for k, v in _L1_xattn_all.items() if k in ('ln_x_g', 'ln_x_b', 'ln_l_g', 'ln_l_b', 'qn_g', 'kn_g', 'Wq', 'Wkv', 'Wlkv', 'Wo', 'bo')}
    del _L1_xattn_all

    def _L1_ffn_setup():
        import jax, jax.numpy as jnp
        import numpy as np
        B, S, D, F, E, K = (2, 1024, 512, 2048, 8, 2)
        key = jax.random.key(seed)
        ks = jax.random.split(key, 5)
        x = jax.random.normal(ks[0], (B, S, D), dtype=jnp.float32)
        Wg = jax.random.normal(ks[1], (D, E), dtype=jnp.float32) * 0.02
        W1 = jax.random.normal(ks[2], (E, D, F), dtype=jnp.float32) * 0.02
        b1 = jnp.zeros((E, F), dtype=jnp.float32)
        W2 = jax.random.normal(ks[3], (E, F, D), dtype=jnp.float32) * 0.02
        b2 = jnp.zeros((E, D), dtype=jnp.float32)
        return {'x': x, 'Wg': Wg, 'W1': W1, 'b1': b1, 'W2': W2, 'b2': b2}
    _L1_ffn_all = _L1_ffn_setup()
    _L1_ffn_in = {k: v for k, v in _L1_ffn_all.items() if k in ('Wg', 'W1', 'b1', 'W2', 'b2')}
    del _L1_ffn_all
    return {'x': x, 'ctx_768': ctx_768, 'mask_BxS_bf1': mask_BxS_bf1, 'mask_BxS2_bf1': mask_BxS2_bf1, 'mask_BxS2_bk0': mask_BxS2_bk0, 'L0_xattn_Wq': _L0_xattn_in['Wq'], 'L0_xattn_Wk': _L0_xattn_in['Wk'], 'L0_xattn_Wv': _L0_xattn_in['Wv'], 'L0_xattn_W_film_in': _L0_xattn_in['W_film_in'], 'L0_xattn_b_film_in': _L0_xattn_in['b_film_in'], 'L0_xattn_W_film_out': _L0_xattn_in['W_film_out'], 'L0_xattn_b_film_out': _L0_xattn_in['b_film_out'], 'L0_xattn_g_norm_in': _L0_xattn_in['g_norm_in'], 'L0_xattn_b_norm_in': _L0_xattn_in['b_norm_in'], 'L0_xattn_g_norm_out': _L0_xattn_in['g_norm_out'], 'L0_xattn_b_norm_out': _L0_xattn_in['b_norm_out'], 'L0_xattn_g_ffn': _L0_xattn_in['g_ffn'], 'L0_xattn_b_ffn': _L0_xattn_in['b_ffn'], 'L0_xattn_W1': _L0_xattn_in['W1'], 'L0_xattn_b1': _L0_xattn_in['b1'], 'L0_xattn_W2': _L0_xattn_in['W2'], 'L0_xattn_b2': _L0_xattn_in['b2'], 'L0_xattn_log_dt': _L0_xattn_in['log_dt'], 'L0_xattn_A_re': _L0_xattn_in['A_re'], 'L0_xattn_A_im': _L0_xattn_in['A_im'], 'L0_xattn_C_re': _L0_xattn_in['C_re'], 'L0_xattn_C_im': _L0_xattn_in['C_im'], 'L0_xattn_D_skip': _L0_xattn_in['D_skip'], 'L0_xattn_mod_gate': _L0_xattn_in['mod_gate'], 'L0_ffn_gate_w': _L0_ffn_in['gate_w'], 'L0_ffn_gate_b': _L0_ffn_in['gate_b'], 'L0_ffn_w1': _L0_ffn_in['w1'], 'L0_ffn_b1': _L0_ffn_in['b1'], 'L0_ffn_w2': _L0_ffn_in['w2'], 'L0_ffn_b2': _L0_ffn_in['b2'], 'L1_xattn_ln_x_g': _L1_xattn_in['ln_x_g'], 'L1_xattn_ln_x_b': _L1_xattn_in['ln_x_b'], 'L1_xattn_ln_l_g': _L1_xattn_in['ln_l_g'], 'L1_xattn_ln_l_b': _L1_xattn_in['ln_l_b'], 'L1_xattn_qn_g': _L1_xattn_in['qn_g'], 'L1_xattn_kn_g': _L1_xattn_in['kn_g'], 'L1_xattn_Wq': _L1_xattn_in['Wq'], 'L1_xattn_Wkv': _L1_xattn_in['Wkv'], 'L1_xattn_Wlkv': _L1_xattn_in['Wlkv'], 'L1_xattn_Wo': _L1_xattn_in['Wo'], 'L1_xattn_bo': _L1_xattn_in['bo'], 'L1_ffn_Wg': _L1_ffn_in['Wg'], 'L1_ffn_W1': _L1_ffn_in['W1'], 'L1_ffn_b1': _L1_ffn_in['b1'], 'L1_ffn_W2': _L1_ffn_in['W2'], 'L1_ffn_b2': _L1_ffn_in['b2']}

def reference(x, ctx_768, mask_BxS_bf1, mask_BxS2_bf1, mask_BxS2_bk0, L0_xattn_Wq, L0_xattn_Wk, L0_xattn_Wv, L0_xattn_W_film_in, L0_xattn_b_film_in, L0_xattn_W_film_out, L0_xattn_b_film_out, L0_xattn_g_norm_in, L0_xattn_b_norm_in, L0_xattn_g_norm_out, L0_xattn_b_norm_out, L0_xattn_g_ffn, L0_xattn_b_ffn, L0_xattn_W1, L0_xattn_b1, L0_xattn_W2, L0_xattn_b2, L0_xattn_log_dt, L0_xattn_A_re, L0_xattn_A_im, L0_xattn_C_re, L0_xattn_C_im, L0_xattn_D_skip, L0_xattn_mod_gate, L0_ffn_gate_w, L0_ffn_gate_b, L0_ffn_w1, L0_ffn_b1, L0_ffn_w2, L0_ffn_b2, L1_xattn_ln_x_g, L1_xattn_ln_x_b, L1_xattn_ln_l_g, L1_xattn_ln_l_b, L1_xattn_qn_g, L1_xattn_kn_g, L1_xattn_Wq, L1_xattn_Wkv, L1_xattn_Wlkv, L1_xattn_Wo, L1_xattn_bo, L1_ffn_Wg, L1_ffn_W1, L1_ffn_b1, L1_ffn_W2, L1_ffn_b2):
    import jax
    import jax.numpy as jnp

    def _L0_xattn_ref(x_text, x_vision, text_mask, vision_mask, Wq, Wk, Wv, W_film_in, b_film_in, W_film_out, b_film_out, g_norm_in, b_norm_in, g_norm_out, b_norm_out, g_ffn, b_ffn, W1, b1, W2, b2, log_dt, A_re, A_im, C_re, C_im, D_skip, mod_gate):
        import jax, jax.numpy as jnp
        import numpy as np
        B, T, DT, G, DV = (16, 256, 512, 288, 384)
        H, DH = (4, 32)
        INNER = H * DH
        HID = 4 * DT
        N_STATE = 64
        K_TOP = 32

        def layernorm(x, g, b, eps=1e-05):
            m = x.mean(-1, keepdims=True)
            v = x.var(-1, keepdims=True)
            return (x - m) * jax.lax.rsqrt(v + eps) * g + b

        def s4d(x, log_dt, A_re, A_im, C_re, C_im, D_skip):
            Bb, L, D = x.shape
            dt = jnp.exp(log_dt)
            A = A_re + 1j * A_im
            C = C_re + 1j * C_im
            dtA = dt[:, None] * A
            dC = C * (jnp.exp(dtA) - 1.0) / A
            powers = jnp.exp(dtA[:, :, None] * jnp.arange(L))
            K = 2.0 * jnp.einsum('dn,dnl->dl', dC, powers).real
            n = 2 * L
            Kf = jnp.fft.rfft(K, n=n, axis=-1)
            xf = jnp.fft.rfft(x, n=n, axis=1)
            y = jnp.fft.irfft(xf * Kf.T[None], n=n, axis=1)[:, :L]
            return y + x * D_skip
        Bb, Tt, D = x_text.shape
        Gg = x_vision.shape[1]
        Q = (x_text @ Wq).reshape(Bb, Tt, H, DH)
        K = (x_vision @ Wk).reshape(Bb, Gg, H, DH)
        scores = jnp.einsum('bthd,bghd->bhtg', Q, K) / np.sqrt(DH).astype(np.float32)
        scores = jnp.where(vision_mask[:, None, None, :], scores, -jnp.inf)
        topv, topi = jax.lax.top_k(scores, K_TOP)
        probs = jax.nn.softmax(topv, axis=-1)
        bi = jnp.arange(Bb)[:, None, None, None]
        hi = jnp.arange(H)[None, :, None, None]
        ti = jnp.arange(Tt)[None, None, :, None]
        attn = jnp.zeros_like(scores).at[bi, hi, ti, topi].set(probs)
        attn_mean = attn.mean(axis=1)
        V = x_vision @ Wv
        c_t = jnp.einsum('btg,bgd->btd', attn_mean, V)
        c_t = c_t * text_mask[..., None]
        x = layernorm(x_text, g_norm_in, b_norm_in)
        scale_in, shift_in = jnp.split(c_t @ W_film_in + b_film_in, 2, axis=-1)
        x = x * (1.0 + mod_gate * scale_in) + mod_gate * shift_in
        y = s4d(x, log_dt, A_re, A_im, C_re, C_im, D_skip)
        scale_out, shift_out = jnp.split(c_t @ W_film_out + b_film_out, 2, axis=-1)
        y = y * (1.0 + mod_gate * scale_out) + mod_gate * shift_out
        xt = x_text + y
        h = layernorm(xt, g_ffn, b_ffn)
        h = jax.nn.gelu(h @ W1 + b1, approximate=False) @ W2 + b2
        xt = xt + h
        return layernorm(xt, g_norm_out, b_norm_out)

    def _L0_ffn_ref(h, gate_w, gate_b, w1, b1, w2, b2):
        import math
        import jax, jax.numpy as jnp
        import numpy as np
        B, L, D, F_FF, E = (4, 1024, 512, 2048, 8)
        TOP_K = 1
        CAPACITY_FACTOR = 1.25
        Bh, Lh, Dh = h.shape
        T = Bh * Lh
        capacity = max(1, math.ceil(CAPACITY_FACTOR * (T * TOP_K / E)))
        x = h.reshape(T, Dh)
        logits = x @ gate_w.T + gate_b
        probs = jax.nn.softmax(logits, axis=-1)
        idx = jnp.argmax(probs, axis=-1)
        top_prob = jnp.max(probs, axis=-1)
        one_hot = jax.nn.one_hot(idx, E, dtype=jnp.int32)
        pos = jnp.take_along_axis(jnp.cumsum(one_hot, axis=0), idx[:, None], axis=1)[:, 0] - 1
        keep = pos < capacity
        safe_pos = jnp.where(keep, pos, 0)
        buf = jnp.zeros((E, capacity, Dh), dtype=x.dtype)
        buf = buf.at[idx, safe_pos].add(x * keep[:, None].astype(x.dtype))
        hdn = jax.nn.relu(jnp.einsum('ecd,edf->ecf', buf, w1) + b1[:, None, :])
        eout = jnp.einsum('ecf,efd->ecd', hdn, w2) + b2[:, None, :]
        gathered = eout[idx, safe_pos]
        out = gathered * (top_prob * keep.astype(x.dtype))[:, None]
        return out.reshape(Bh, Lh, Dh)

    def _L1_xattn_ref(x, latents, mask, ln_x_g, ln_x_b, ln_l_g, ln_l_b, qn_g, kn_g, Wq, Wkv, Wlkv, Wo, bo):
        import jax, jax.numpy as jnp
        import numpy as np
        DIM_IN, DIM_LAT, DIM_HEAD = (384, 512, 64)
        INNER = max(DIM_LAT, DIM_IN)
        HEADS = INNER // DIM_HEAD
        SCALE = DIM_HEAD ** (-0.5)
        RMS_EPS = 1e-08
        LN_EPS = 1e-05

        def layernorm(x, g, b):
            mu = jnp.mean(x, axis=-1, keepdims=True)
            var = jnp.mean((x - mu) ** 2, axis=-1, keepdims=True)
            return (x - mu) * jax.lax.rsqrt(var + LN_EPS) * g + b

        def rmsnorm(x, gamma):
            norm = jnp.sqrt(jnp.sum(x * x, axis=-1, keepdims=True)) * x.shape[-1] ** (-0.5)
            return x / jnp.maximum(norm, RMS_EPS) * gamma
        b, n, _ = x.shape
        m = latents.shape[1]
        xn = layernorm(x, ln_x_g, ln_x_b)
        ln = layernorm(latents, ln_l_g, ln_l_b)
        q = ln @ Wq.T
        kv = jnp.concatenate([xn @ Wkv.T, ln @ Wlkv.T], axis=1)
        k, v = (kv[..., :INNER], kv[..., INNER:])
        split_heads = lambda t: t.reshape(t.shape[0], t.shape[1], HEADS, DIM_HEAD).transpose(0, 2, 1, 3)
        q, k, v = (split_heads(q), split_heads(k), split_heads(v))
        qn = rmsnorm(q, qn_g) * SCALE
        kn = rmsnorm(k, kn_g)
        attn = jnp.einsum('bhid,bhjd->bhij', qn, kn)
        full_mask = jnp.pad(mask, ((0, 0), (0, m)), constant_values=True)
        attn = jnp.where(full_mask[:, None, None, :], attn, -jnp.finfo(attn.dtype).max)
        attn = jax.nn.softmax(attn, axis=-1)
        out = jnp.einsum('bhij,bhjd->bhid', attn, v)
        out = out.transpose(0, 2, 1, 3).reshape(b, m, INNER)
        return out @ Wo.T + bo

    def _L1_ffn_ref(x, Wg, W1, b1, W2, b2):
        import jax, jax.numpy as jnp
        import numpy as np
        B, S, D, F, E, K = (2, 1024, 512, 2048, 8, 2)
        b, s, d = x.shape
        e = Wg.shape[1]
        T = b * s
        C = 2 * K * T // e
        xt = x.reshape(T, d)
        logits = xt.astype(jnp.float32) @ Wg.astype(jnp.float32)
        gates = jax.nn.softmax(logits, axis=-1)
        idx1 = jnp.argmax(gates, axis=-1)
        mask1 = jax.nn.one_hot(idx1, e, dtype=gates.dtype)
        gate1 = jnp.sum(gates * mask1, axis=-1)
        logits2 = jnp.where(mask1 > 0, -jnp.inf, logits)
        idx2 = jnp.argmax(logits2, axis=-1)
        mask2 = jax.nn.one_hot(idx2, e, dtype=gates.dtype)
        gate2 = jnp.sum(gates * mask2, axis=-1)
        denom = gate1 + gate2 + 1e-09
        w1 = gate1 / denom
        w2 = gate2 / denom
        p1 = jnp.cumsum(mask1, axis=0) - mask1
        pos1 = jnp.sum(p1 * mask1, axis=-1).astype(jnp.int32)
        off = jnp.sum(mask1, axis=0)
        p2 = jnp.cumsum(mask2, axis=0) - mask2 + off[None, :]
        pos2 = jnp.sum(p2 * mask2, axis=-1).astype(jnp.int32)
        keep1 = (pos1 < C).astype(xt.dtype)
        keep2 = (pos2 < C).astype(xt.dtype)
        pos1 = jnp.clip(pos1, 0, C - 1)
        pos2 = jnp.clip(pos2, 0, C - 1)
        xe = jnp.zeros((e, C, d), dtype=xt.dtype)
        xe = xe.at[idx1, pos1].add(xt * keep1[:, None])
        xe = xe.at[idx2, pos2].add(xt * keep2[:, None])
        h = jax.nn.gelu(jnp.einsum('ecd,edf->ecf', xe, W1) + b1[:, None, :], approximate=False)
        ye = jnp.einsum('ecf,efd->ecd', h, W2) + b2[:, None, :]
        out = ye[idx1, pos1] * (w1 * keep1)[:, None] + ye[idx2, pos2] * (w2 * keep2)[:, None]
        return out.reshape(b, s, d)
    x = x + _L0_xattn_ref(_layernorm(x, axis=-1), ctx_768, mask_BxS_bf1, mask_BxS2_bf1, L0_xattn_Wq, L0_xattn_Wk, L0_xattn_Wv, L0_xattn_W_film_in, L0_xattn_b_film_in, L0_xattn_W_film_out, L0_xattn_b_film_out, L0_xattn_g_norm_in, L0_xattn_b_norm_in, L0_xattn_g_norm_out, L0_xattn_b_norm_out, L0_xattn_g_ffn, L0_xattn_b_ffn, L0_xattn_W1, L0_xattn_b1, L0_xattn_W2, L0_xattn_b2, L0_xattn_log_dt, L0_xattn_A_re, L0_xattn_A_im, L0_xattn_C_re, L0_xattn_C_im, L0_xattn_D_skip, L0_xattn_mod_gate)
    x = x + _L0_ffn_ref(_layernorm(x, axis=-1), L0_ffn_gate_w, L0_ffn_gate_b, L0_ffn_w1, L0_ffn_b1, L0_ffn_w2, L0_ffn_b2)
    x = x + _L1_xattn_ref(ctx_768, _layernorm(x, axis=-1), mask_BxS2_bk0, L1_xattn_ln_x_g, L1_xattn_ln_x_b, L1_xattn_ln_l_g, L1_xattn_ln_l_b, L1_xattn_qn_g, L1_xattn_kn_g, L1_xattn_Wq, L1_xattn_Wkv, L1_xattn_Wlkv, L1_xattn_Wo, L1_xattn_bo)
    x = x + _L1_ffn_ref(_layernorm(x, axis=-1), L1_ffn_Wg, L1_ffn_W1, L1_ffn_b1, L1_ffn_W2, L1_ffn_b2)
    return x

_drawn_inputs = setup_inputs


def setup_inputs(seed=0):
    import zlib

    import numpy as np

    out = dict(_drawn_inputs(seed))
    spreads = {'L0_xattn_b_film_in': (0.0, 0.1),
     'L0_xattn_b_film_out': (0.0, 0.1),
     'L0_xattn_g_norm_in': (1.0, 0.2),
     'L0_xattn_b_norm_in': (0.0, 0.1),
     'L0_xattn_g_norm_out': (1.0, 0.2),
     'L0_xattn_b_norm_out': (0.0, 0.1),
     'L0_xattn_g_ffn': (1.0, 0.6),
     'L0_xattn_b_ffn': (0.0, 0.8),
     'L0_xattn_b1': (0.0, 0.337),
     'L0_xattn_b2': (0.0, 0.1),
     'L0_xattn_A_re': (-0.5, 0.2),
     'L0_ffn_gate_b': (0.0, 0.32),
     'L0_ffn_b1': (0.0, 0.728),
     'L0_ffn_b2': (0.0, 0.474),
     'L1_xattn_ln_x_g': (1.0, 0.6),
     'L1_xattn_ln_x_b': (0.0, 0.413),
     'L1_xattn_ln_l_g': (1.0, 0.2),
     'L1_xattn_ln_l_b': (0.0, 0.1),
     'L1_xattn_qn_g': (1.0, 0.6),
     'L1_xattn_kn_g': (1.0, 0.6),
     'L1_xattn_bo': (0.0, 0.1),
     'L1_ffn_b1': (0.0, 0.384),
     'L1_ffn_b2': (0.0, 0.1)}
    factors = {}
    for name, (base, spread) in spreads.items():
        noise = np.random.default_rng([zlib.crc32(name.encode()), seed]).standard_normal(out[name].shape)
        drawn = base * np.exp(spread * noise) if base else spread * noise
        out[name] = jnp.asarray(drawn.astype(out[name].dtype))
    for name, factor in factors.items():
        out[name] = (out[name] * factor).astype(out[name].dtype)
    return out
```

```python
from contextlib import ExitStack

import numpy as np

import concourse.bass as bass
from concourse import mybir

F32 = mybir.dt.float32
I32 = mybir.dt.int32
U8 = mybir.dt.uint8
ACT = mybir.ActivationFunctionType
ALU = mybir.AluOpType
AX = mybir.AxisListType

B, T, D = 8, 100, 512
NTOK = B * T
JCTX = J = 722
DC = 384
KD, KJ, KC = D // 128, (J + 127) // 128, DC // 128
JTAIL = J - 128 * (KJ - 1)
H0, DH0, TOPK = 4, 32, 32
H1, DH1 = 8, 64
JNEAR = 2 * 128
FF, KF = 2048, 16
E, CAP0, CAP1 = 8, 125, 400
WIDTHS = (128, 160, 192, 240, 288, 400)
NS = 64
NFREQ = T + 1
LB = 4
LA = T // LB
FLOOR = -1.0e30
GONE = -3.0e38
ROUND = 12582912.0


class Steps:

    def __init__(self, sem, names, ahead=0):
        self.sem, self.names, self.ahead = sem, list(names), ahead
        self.value = {n: k + 1 for k, n in enumerate(self.names)}
        assert len(self.value) == len(self.names)
        self.next = 0

    def __call__(self, name, rnd=0):
        return self.sem, (rnd + self.ahead) * len(self.names) + self.value[name]

    def done(self, name):
        assert self.names[self.next % len(self.names)] == name, (name, self.names[self.next % len(self.names)])
        self.next += 1
        return self.sem, 1


def bc(ap, shape):
    return ap.to_broadcast(shape)


def over_b(row, n=B):
    p, d = row.shape
    return row.rearrange("p (o d) -> p o d", o=1).to_broadcast((p, n, d))


def over_d(col, d):
    p, n = col.shape
    return col.rearrange("p (n o) -> p n o", o=1).to_broadcast((p, n, d))


def row_bcast(vec, p):
    (n,) = vec.shape
    return vec.rearrange("(o n) -> o n", o=1).to_broadcast((p, n))


def norm_vec_names(pre, affine):
    names = [f"{pre}stats{b}" for b in range(B)] + [f"{pre}mean{b}" for b in range(B)] + [f"{pre}rstd"]
    names += [f"{pre}centred{b}" for b in range(B)]
    if affine:
        names += [f"{pre}scaled{b}" for b in range(B)] + [f"{pre}shifted{b}" for b in range(B)]
    return names


def norm_last(affine):
    return "shifted" if affine else "centred"


def norm_vector(dve, pre, V, A, src, dst, st, mv, rs, gain=None, shift=None):
    for b in range(B):
        dve.bn_stats(st[:, b, :], src[:, b, :]).then_inc(*V.done(f"{pre}stats{b}"))
    for b in range(B):
        dve.wait_ge(*V(f"{pre}stats{b}"))
        dve.bn_aggr(mv[:, b, :], st[:, b, :]).then_inc(*V.done(f"{pre}mean{b}"))
    dve.wait_ge(*A(f"{pre}std"))
    dve.reciprocal(rs[:, 1, :], rs[:, 0, :]).then_inc(*V.done(f"{pre}rstd"))
    dve.wait_ge(*V(f"{pre}rstd"))
    for b in range(B):
        dve.tensor_scalar(dst[:, b, :], src[:, b, :], mv[:, b, 0:1], rs[:, 1, b:b + 1],
                          ALU.subtract, ALU.mult).then_inc(*V.done(f"{pre}centred{b}"))
    if gain is not None:
        for b in range(B):
            dve.wait_ge(*V(f"{pre}centred{b}"))
            dve.tensor_tensor(dst[:, b, :], dst[:, b, :], gain, ALU.mult).then_inc(*V.done(f"{pre}scaled{b}"))
        for b in range(B):
            dve.wait_ge(*V(f"{pre}scaled{b}"))
            dve.tensor_tensor(dst[:, b, :], dst[:, b, :], shift, ALU.add).then_inc(*V.done(f"{pre}shifted{b}"))


def norm_scalar(act, pre, V, A, mv, rs, eps):
    act.wait_ge(*V(f"{pre}mean{B - 1}"))
    act.activation(rs[:, 0, :], mv[:, :, 1], ACT.Sqrt, bias=eps[0:T, 0:1]).then_inc(*A.done(f"{pre}std"))


def turn_names():
    return [f"turned{b}" for b in range(B)]


def turn_tensor(pe, P, A, ready, src, ps, ident):
    for b in range(B):
        pe.wait_ge(*ready(b))
        if b >= 2:
            pe.wait_ge(*A(f"turned{b - 2}"))
        for k in range(KD):
            ins = pe.transpose(ps[:, b % 2, k * T:(k + 1) * T], src[:, b, k * 128:(k + 1) * 128], ident[0:T, 0:T])
        ins.then_inc(*P.done(f"turned{b}"))


def turn_scalar(act, P, A, ps, dst):
    for b in range(B):
        act.wait_ge(*P(f"turned{b}"))
        act.activation(dst[:, :, b * T:(b + 1) * T], ps[:, b % 2, 0:KD * T].rearrange("p (k t) -> p k t", k=KD),
                       ACT.Copy).then_inc(*A.done(f"turned{b}"))


class Core:

    def __init__(self, nc, ctx, stage):
        self.nc, self.ctx, self.stage = nc, ctx, stage

    def sb(self, name, shape, dt=F32):
        return self.ctx.enter_context(self.nc.sbuf_tensor(f"{self.stage}_{name}", shape, dt))

    def ps(self, name, shape, dt=F32):
        return self.ctx.enter_context(self.nc.psum_tensor(f"{self.stage}_{name}", shape, dt))

    def sem(self, name):
        return self.ctx.enter_context(self.nc.semaphore(f"{self.stage}_{name}"))

    def block(self):
        return self.ctx.enter_context(self.nc.Block())


def stage_s4d_kernel(nc, I, G):
    with ExitStack() as ctx:
        c = Core(nc, ctx, "kern")
        ND = D // 128
        logdt, dt = c.sb("logdt", [128, ND]), c.sb("dt", [128, ND])
        Are, Aim, Cre, Cim = (c.sb(n, [128, ND, NS]) for n in ("Are", "Aim", "Cre", "Cim"))
        R, TH, EX = (c.sb(n, [128, ND, NS]) for n in ("R", "TH", "EX"))
        K1, K2, SI, CO = (c.sb(n, [128, ND, NS]) for n in ("K1", "K2", "SI", "CO"))
        Z = c.sb("Z", [128, 2, ND, NS])
        dC = c.sb("dC", [128, 2, ND, NS])
        W = [c.sb(f"W{i}", [128, ND, NS]) for i in range(6)]
        Q = c.sb("Q", [128, LA, 2, NS])
        PW = c.sb("PW", [128, 8, 2, NS])
        Z64 = c.sb("Z64", [128, 2, NS])
        T4 = [c.sb(f"T{i}", [128, LA, NS]) for i in range(4)]
        QT = c.sb("QT", [128, 32, 4, 32])
        PT = c.sb("PT", [128, LB, 128])
        KK = c.sb("KK", [128, ND, 32, 4, LB])
        dft = c.sb("dft", [128, LB, 2, NFREQ])
        skip = c.sb("skip", [NFREQ, D])
        zeros = c.sb("zeros", [128, 4096])
        far8, farf = c.sb("far8", [1, B, J - JNEAR], U8), c.sb("farf", [1, 1])
        halfpi = c.sb("halfpi", [128, 1])
        pq = c.ps("pq", [128, 4, 512])
        pk = c.ps("pk", [128, 512])

        s_far = c.sem("far_mask_in")
        s_in, s_par, s_z, s_dft = c.sem("inputs_in"), c.sem("params_in"), c.sem("zero_fill"), c.sem("dft_in")
        GN = ["zeros", "halfpi", "qt0"]
        P0 = Steps(c.sem("pool_consts"), GN)
        VN = (["re", "im", "turns_s", "round_s", "red_s1", "red_s2", "clip_s", "turns_c", "round_c", "red_c1", "red_c2",
               "add_c", "clip_c", "z_re", "z_im", "zm1"]
              + [f"n{i}" for i in range(6)] + [f"a{i}" for i in range(3)] + ["inv"] + [f"m{i}" for i in range(2)]
              + [f"c{i}" for i in range(6)] + ["far", "far_i"])
        V = Steps(c.sem("vector"), VN)
        A = Steps(c.sem("scalar"), ["dt", "ex", "sin", "cos"])

        def cmul(name):
            return [f"{name}_{i}" for i in range(6)]

        LN = ["p0", "p0b", "p1", "p1b", "q0"]
        for n in ("z2", "z3", "z4", "z8", "z16", "z32", "z64", "d1", "d2", "d4", "d8", "d16"):
            LN += cmul(n)
        LN += ["neg"]
        VL = Steps(c.sem("powers"), LN, ahead=1)
        NQ = (LA + 3) // 4
        PL = Steps(c.sem("table_turn"), [f"q{i}" for i in range(NQ)] + ["p", "k"], ahead=1)
        AL = Steps(c.sem("table_copy"), [f"q{i}" for i in range(NQ)] + ["p", "k"], ahead=1)
        PF = Steps(c.sem("transform"), ["f"])
        VF = Steps(c.sem("response"), ["kr", "ki"])
        block = c.block()

        @block.sync
        def _(sp):
            sp.dma_start(G.X[:], I["x"].rearrange("b t d -> t b d")).then_inc(s_in, 16)
            sp.dma_start(logdt[:], I["log_dt"]).then_inc(s_par, 16)
            for t, n in ((Are, "A_re"), (Aim, "A_im"), (Cre, "C_re"), (Cim, "C_im")):
                sp.dma_start(t[:], I[n].rearrange("(t p) n -> p t n", p=128)).then_inc(s_par, 16)
            sp.dma_start(G.ident[:], I["ident"]).then_inc(s_in, 16)
            sp.dma_start(dft[:], I["dft_fold"]).then_inc(s_dft, 16)
            sp.dma_start(skip[:], row_bcast(I["D_skip"], NFREQ)).then_inc(s_dft, 16)
            sp.dma_start(far8[:], I["kmask"][:, 0:J - JNEAR].rearrange("(o b) j -> o b j", o=1)).then_inc(s_far, 16)
            sp.wait_ge(*P0("zeros"))
            n = 0
            for dst, rows in ((G.xe0, E * CAP0), (G.xe1, E * CAP1)):
                flat = dst[0:rows, :].rearrange("(p r) d -> p (r d)", p=125 if rows == 1000 else 128)
                w = flat.shape[1]
                for o in range(0, w, 4096):
                    m = min(4096, w - o)
                    sp.dma_start(flat[:, o:o + m], zeros[0:flat.shape[0], 0:m]).then_inc(s_z, 16)
                    n += 1
            sp.wait_ge(s_z, 16 * n)
            sp.wait_ge(s_in, 32)

        @block.gpsimd
        def _(pool):
            pool.memset(zeros[:], 0.0).then_inc(*P0.done("zeros"))
            pool.memset(halfpi[:], 1.0e-5).then_inc(*P0.done("halfpi"))
            pool.memset(QT[:, :, :, LA:32], 0.0).then_inc(*P0.done("qt0"))
            pool.memset(G.eps[:], 1.0e-5)

        @block.scalar
        def _(act):
            act.wait_ge(s_par, 80)
            act.activation(dt[:], logdt[:], ACT.Exp).then_inc(*A.done("dt"))
            act.wait_ge(*V("re"))
            act.activation(EX[:], R[:], ACT.Exp).then_inc(*A.done("ex"))
            act.wait_ge(*V("clip_s"))
            act.activation(SI[:], K1[:], ACT.Sin).then_inc(*A.done("sin"))
            act.wait_ge(*V("clip_c"))
            act.activation(CO[:], K2[:], ACT.Sin).then_inc(*A.done("cos"))
            act.sem_inc(AL.sem, len(AL.names))
            act.wait_ge(*P0("qt0"))
            with act.Fori(0, ND) as t:
                for i in range(NQ):
                    n = min(4, LA - 4 * i)
                    act.wait_ge(*PL(f"q{i}", t))
                    act.activation(QT[:, :, :, 4 * i:4 * i + n].rearrange("p g e a -> p a e g"),
                                   pq[:, i % 3, 0:n * 128].rearrange("p (a e g) -> p a e g", a=n, e=4),
                                   ACT.Copy).then_inc(*AL.done(f"q{i}"))
                act.wait_ge(*PL("p", t))
                act.activation(PT[:], pq[:, 3, :].rearrange("p (a d) -> p a d", a=LB),
                               ACT.Copy).then_inc(*AL.done("p"))
                act.wait_ge(*PL("k", t))
                act.activation(KK[:, bass.ds(t, 1), :, :, :].rearrange("p o g e b -> p (o g e b)"), pk[:],
                               ACT.Copy).then_inc(*AL.done("k"))

        @block.vector
        def _(dve):
            tt, ts, stt = dve.tensor_tensor, dve.tensor_scalar, dve.scalar_tensor_tensor
            C1, C2 = 6.28125, float(2 * np.pi - 6.28125)
            dve.wait_ge(*A("dt"))
            tt(R[:], Are[:], over_d(dt[:], NS), ALU.mult).then_inc(*V.done("re"))
            tt(TH[:], Aim[:], over_d(dt[:], NS), ALU.mult).then_inc(*V.done("im"))

            for k, dst, quarter in (("s", K1, 0.0), ("c", K2, 0.25)):
                dve.wait_ge(*V("im"))
                ts(dst[:], TH[:], float(1 / (2 * np.pi)), quarter, ALU.mult, ALU.add).then_inc(*V.done(f"turns_{k}"))
                dve.wait_ge(*V(f"turns_{k}"))
                ts(dst[:], dst[:], ROUND, -ROUND, ALU.add, ALU.add).then_inc(*V.done(f"round_{k}"))
                dve.wait_ge(*V(f"round_{k}"))
                w = W[0] if k == "s" else W[1]
                stt(w[:], dst[:], -C1, TH[:], ALU.mult, ALU.add).then_inc(*V.done(f"red_{k}1"))
                dve.wait_ge(*V(f"red_{k}1"))
                stt(dst[:], dst[:], -C2, w[:], ALU.mult, ALU.add).then_inc(*V.done(f"red_{k}2"))
                dve.wait_ge(*V(f"red_{k}2"))
                if k == "c":
                    ts(dst[:], dst[:], float(np.pi / 2), None, ALU.add).then_inc(*V.done("add_c"))
                    dve.wait_ge(*V("add_c"))
                ts(dst[:], dst[:], 3.1415925, -3.1415925, ALU.min, ALU.max).then_inc(*V.done(f"clip_{k}"))
            dve.wait_ge(*A("cos"))
            tt(Z[:, 0], EX[:], CO[:], ALU.mult).then_inc(*V.done("z_re"))
            tt(Z[:, 1], EX[:], SI[:], ALU.mult).then_inc(*V.done("z_im"))
            dve.wait_ge(*V("z_im"))
            ts(W[0][:], Z[:, 0], -1.0, None, ALU.add).then_inc(*V.done("zm1"))
            dve.wait_ge(*V("zm1"))
            tt(W[1][:], W[0][:], Are[:], ALU.mult).then_inc(*V.done("n0"))
            tt(W[2][:], Z[:, 1], Aim[:], ALU.mult).then_inc(*V.done("n1"))
            tt(W[3][:], Z[:, 1], Are[:], ALU.mult).then_inc(*V.done("n2"))
            tt(W[4][:], W[0][:], Aim[:], ALU.mult).then_inc(*V.done("n3"))
            dve.wait_ge(*V("n3"))
            tt(W[1][:], W[1][:], W[2][:], ALU.add).then_inc(*V.done("n4"))
            tt(W[3][:], W[3][:], W[4][:], ALU.subtract).then_inc(*V.done("n5"))
            tt(W[0][:], Are[:], Are[:], ALU.mult).then_inc(*V.done("a0"))
            tt(W[5][:], Aim[:], Aim[:], ALU.mult).then_inc(*V.done("a1"))
            dve.wait_ge(*V("a1"))
            tt(W[0][:], W[0][:], W[5][:], ALU.add).then_inc(*V.done("a2"))
            dve.wait_ge(*V("a2"))
            dve.reciprocal(W[5][:], W[0][:]).then_inc(*V.done("inv"))
            dve.wait_ge(*V("inv"))
            stt(W[1][:], W[1][:], 2.0, W[5][:], ALU.mult, ALU.mult).then_inc(*V.done("m0"))
            stt(W[3][:], W[3][:], 2.0, W[5][:], ALU.mult, ALU.mult).then_inc(*V.done("m1"))
            dve.wait_ge(*V("m1"))
            tt(W[0][:], W[1][:], Cre[:], ALU.mult).then_inc(*V.done("c0"))
            tt(W[2][:], W[3][:], Cim[:], ALU.mult).then_inc(*V.done("c1"))
            tt(W[4][:], W[1][:], Cim[:], ALU.mult).then_inc(*V.done("c2"))
            tt(W[5][:], W[3][:], Cre[:], ALU.mult).then_inc(*V.done("c3"))
            dve.wait_ge(*V("c3"))
            tt(dC[:, 0], W[0][:], W[2][:], ALU.subtract).then_inc(*V.done("c4"))
            tt(dC[:, 1], W[4][:], W[5][:], ALU.add).then_inc(*V.done("c5"))
            dve.wait_ge(s_far, 16)
            dve.tensor_reduce(farf[:], far8[:], AX.XY, ALU.max).then_inc(*V.done("far"))
            dve.wait_ge(*V("far"))
            dve.tensor_copy(G.far[:], farf[:]).then_inc(*V.done("far_i"))

            dve.sem_inc(VL.sem, len(VL.names))
            with dve.Fori(0, ND) as t:
                def step(ins, name):
                    ins.then_inc(*VL.done(name))
                    dve.wait_ge(*VL(name, t))

                def z(ch):
                    return Z[:, ch, bass.ds(t, 1), :].rearrange("p o n -> p (o n)")

                def mul(name, out, x, y, k=1):
                    def rows(a):
                        return a
                    yb = [y[i] if k == 1 else y[i].rearrange("p (o n) -> p o n", o=1).to_broadcast((128, k, NS))
                          for i in range(2)]
                    t4 = [T4[i][:, 0, :] if k == 1 else T4[i][:, 0:k, :] for i in range(4)]
                    for i, (u, v) in enumerate(((0, 0), (1, 1), (0, 1), (1, 0))):
                        ins = tt(t4[i], x[u], yb[v], ALU.mult)
                        if i < 3:
                            ins.then_inc(*VL.done(f"{name}_{i}"))
                        else:
                            step(ins, f"{name}_{i}")
                    tt(out[0], t4[0], t4[1], ALU.subtract).then_inc(*VL.done(f"{name}_4"))
                    step(tt(out[1], t4[2], t4[3], ALU.add), f"{name}_5")

                dve.wait_ge(*PL("p", t - 1))
                dve.memset(PW[:, 0, 0, :], 1.0).then_inc(*VL.done("p0"))
                dve.memset(PW[:, 0, 1, :], 0.0).then_inc(*VL.done("p0b"))
                dve.tensor_copy(PW[:, 1, 0, :], z(0)).then_inc(*VL.done("p1"))
                dve.tensor_copy(PW[:, 1, 1, :], z(1)).then_inc(*VL.done("p1b"))
                step(dve.tensor_copy(Q[:, 0, :, :], dC[:, :, bass.ds(t, 1), :].rearrange("p c o n -> p c (o n)")), "q0")
                pw = lambda i: (PW[:, i, 0, :], PW[:, i, 1, :])
                q = lambda a, n: (Q[:, a:a + n, 0, :], Q[:, a:a + n, 1, :]) if n > 1 else (Q[:, a, 0, :], Q[:, a, 1, :])
                mul("z2", pw(2), pw(1), pw(1))
                mul("z3", pw(3), pw(2), pw(1))
                mul("z4", pw(4), pw(2), pw(2))
                mul("z8", pw(5), pw(4), pw(4))
                mul("z16", pw(6), pw(5), pw(5))
                mul("z32", pw(7), pw(6), pw(6))
                mul("z64", (Z64[:, 0, :], Z64[:, 1, :]), pw(7), pw(7))
                mul("d1", q(1, 1), q(0, 1), pw(4))
                mul("d2", q(2, 2), q(0, 2), pw(5), 2)
                mul("d4", q(4, 4), q(0, 4), pw(6), 4)
                mul("d8", q(8, 8), q(0, 8), pw(7), 8)
                mul("d16", q(16, LA - 16), q(0, LA - 16), (Z64[:, 0, :], Z64[:, 1, :]), LA - 16)
                step(ts(PW[:, 0:4, 1, :], PW[:, 0:4, 1, :], -1.0, None, ALU.mult), "neg")
            dve.wait_ge(*PF("f"))
            dve.wait_ge(s_dft, 32)
            for ch, name in ((0, "kr"), (1, "ki")):
                dst = G.Kf[:, ch, :].rearrange("p (t e g) -> p t e g", t=ND, e=4)
                src = pq[0:NFREQ, :, ch * 128:(ch + 1) * 128].rearrange("p e (t g) -> p t e g", t=ND)
                for tq in range(ND):
                    if ch == 0:
                        ins = tt(dst[:, tq], src[:, tq], skip[:].rearrange("p (t e g) -> p t e g", t=ND, e=4)[:, tq],
                                 ALU.add)
                    else:
                        ins = dve.tensor_copy(dst[:, tq], src[:, tq])
                ins.then_inc(*VF.done(name))

        @block.tensor
        def _(pe):
            pe.sem_inc(PL.sem, len(PL.names))
            pe.wait_ge(s_in, 32)
            with pe.Fori(0, ND) as t:
                pe.wait_ge(*VL("neg", t))
                for i in range(NQ):
                    if i < 3:
                        pe.wait_ge(*AL("k", t - 1))
                    else:
                        pe.wait_ge(*AL(f"q{i - 3}", t))
                    for a in range(4 * i, min(4 * i + 4, LA)):
                        ins = pe.transpose(pq[:, i % 3, (a % 4) * 128:(a % 4 + 1) * 128], Q[:, a, :, :].rearrange("p c n -> p (c n)"), G.ident[:])
                    ins.then_inc(*PL.done(f"q{i}"))
                for b in range(LB):
                    ins = pe.transpose(pq[:, 3, b * 128:(b + 1) * 128],
                                       PW[:, b, :, :].rearrange("p c n -> p (c n)"), G.ident[:])
                ins.then_inc(*PL.done("p"))
                pe.wait_ge(*AL("p", t))
                pt = PT[:].rearrange("p b (e g) -> p e b g", e=4)
                for g in range(32):
                    ins = pe.matmul(pk[:, g * 16:(g + 1) * 16], QT[:, g, :, :].rearrange("p e a -> p (e a)"), pt[:, :, :, g], start=True, stop=True)
                ins.then_inc(*PL.done("k"))
            pe.wait_ge(s_dft, 32)
            pe.wait_ge(*AL("k", ND - 1))
            for ch in range(2):
                for e in range(4):
                    rows = slice(32 * e, 32 * e + 32)
                    for b in range(LB):
                        ins = pe.matmul(pq[0:NFREQ, e, ch * 128:(ch + 1) * 128], dft[rows, b, ch, :],
                                        KK[rows, :, :, e, b], start=b == 0, stop=b == LB - 1)
            ins.then_inc(*PF.done("f"))


def stage_topk_attention(nc, I, G):
    with ExitStack() as ctx:
        c = Core(nc, ctx, "topk")
        st, mv, rs = c.sb("st", [T, B, 6]), c.sb("mv", [T, B, 2]), c.sb("rs", [T, 2, B])
        Wq, Wk = c.sb("Wq", [128, KD, 128]), c.sb("Wk", [128, KC, 128])
        QT, QTb = c.sb("QT", [128, NTOK]), c.sb("QTb", [128, T])
        CT, CR = c.sb("CT", [128, KC, J]), c.sb("CR", [128, KJ, DC])
        KT = c.sb("KT", [128, J])
        S, R = c.sb("S", [T, H0, J]), c.sb("R", [T, H0, J])
        M = c.sb("M", [T, H0, TOPK])
        ME = c.sb("ME", [T, TOPK])
        nmx, Zs, rz = c.sb("nmx", [T, H0]), c.sb("Zs", [T, H0]), c.sb("rz", [T, H0])
        mask8, maskf = c.sb("mask8", [T, J], U8), c.sb("maskf", [T, J])
        tm8, tmq = c.sb("tm8", [T, B], U8), c.sb("tmq", [T, B])
        diag = c.sb("diag", [T, H0, T])
        AT = c.sb("AT", [128, KJ, T])
        pt = c.ps("pt", [128, 2, 512])
        pk = c.ps("pk", [128, 2, 512])
        pss = c.ps("pss", [128, 2, 2, 512])
        XT = G.XT
        s_here = c.sem("waits_met")
        s_w, s_ct, s_cr, s_m, s_tm = (c.sem(n) for n in ("weights_in", "ctxT_in", "ctx_in", "mask_in", "tmask_in"))
        V = Steps(c.sem("norm"), norm_vec_names("", False) + ["tmf", "tmq"])
        P = Steps(c.sem("x_turned"), turn_names() + ["q0", "q1"])
        A = Steps(c.sem("x_copied"), ["std"] + turn_names() + ["q0", "q1"])
        heads = range(H0)
        PL = Steps(c.sem("pe_loop"), ["k"] + [f"s{h}" for h in heads] + ["a", "c"], ahead=1)
        AL = Steps(c.sem("act_loop"), ["q", "k0", "k1"] + [f"s{h}" for h in heads]
                   + [f"{n}{h}" for h in heads for n in ("e1", "e2", "z")] + ["a", "a5", "c"], ahead=1)
        VL = Steps(c.sem("dve_loop"), ["mf", "mb"]
                   + [f"{n}{h}" for h in heads for n in ("m0", "r0", "m1", "r1", "m2", "r2", "m3", "r3", "n")]
                   + [f"{n}{h}" for h in heads for n in ("rz", "w", "d")], ahead=1)
        GL = Steps(c.sem("pool_loop"), [f"m{h}" for h in heads] + [f"d{h}" for h in heads], ahead=1)
        block = c.block()

        @block.sync
        def _(sp):
            sp.dma_start(Wq[:], I["L0_Wq"].rearrange("(k p) n -> p k n", p=128)).then_inc(s_w, 16)
            sp.dma_start(Wk[:], I["L0_Wk"].rearrange("(k p) n -> p k n", p=128)).then_inc(s_w, 16)
            sp.dma_start(tm8[:], I["tmask"]).then_inc(s_tm, 16)
            with sp.Fori(0, B) as b:
                sp.wait_ge(*PL("k", b - 1))
                sp.dma_start(CT[:], I["ctxT"][bass.ds(b, 1), :, :].rearrange("o (k p) j -> p (o k) j", p=128)).then_inc(s_ct, 16)
                sp.wait_ge(*VL("mf", b - 1))
                sp.sem_inc(s_here, 1)
                sp.dma_start(mask8[:], I["vmask"][bass.ds(b, 1), :].to_broadcast((T, J))).then_inc(s_m, 16)
                sp.wait_ge(*PL("c", b - 1))
                rows = I["ctx"][bass.ds(b, 1), :, :].rearrange("o j c -> (o j) c")
                sp.dma_start(CR[:, 0:KJ - 1, :], rows[0:128 * (KJ - 1), :].rearrange("(k p) c -> p k c", p=128)).then_inc(s_cr, 16)
                sp.dma_start(CR[0:JTAIL, KJ - 1, :], rows[128 * (KJ - 1):J, :]).then_inc(s_cr, 16)

        @block.gpsimd
        def _(pool):
            pool.sem_inc(GL.sem, len(GL.names))
            with pool.Fori(0, B) as b:
                pool.wait_ge(*VL("mb", b))
                for h in heads:
                    pool.wait_ge(*AL(f"s{h}", b))
                    pool.tensor_tensor(S[:, h, :], S[:, h, :], maskf[:], ALU.add).then_inc(*GL.done(f"m{h}"))
                for h in heads:
                    pool.wait_ge(*AL(f"e2{h}", b))
                    pool.tensor_tensor(S[:, h, :], S[:, h, :], R[:, h, :], ALU.subtract).then_inc(*GL.done(f"d{h}"))

        @block.vector
        def _(dve):
            norm_vector(dve, "", V, A, G.X, G.N, st, mv, rs)
            dve.wait_ge(s_tm, 16)
            dve.tensor_copy(tmq[:], tm8[:]).then_inc(*V.done("tmf"))
            dve.wait_ge(*V("tmf"))
            dve.tensor_scalar(tmq[:], tmq[:], 1.0 / H0, None, ALU.mult).then_inc(*V.done("tmq"))
            dve.wait_ge(*V("tmq"))
            dve.sem_inc(VL.sem, len(VL.names))
            with dve.Fori(0, B) as b:
                dve.wait_ge(s_m, 16 * b + 16)
                dve.wait_ge(*GL(f"m{H0 - 1}", b - 1))
                dve.tensor_copy(maskf[:], mask8[:]).then_inc(*VL.done("mf"))
                dve.wait_ge(*VL("mf", b))
                dve.tensor_scalar(maskf[:], maskf[:], -1.0, -FLOOR, ALU.add, ALU.mult).then_inc(*VL.done("mb"))
                for h in heads:
                    dve.wait_ge(*GL(f"m{h}", b))
                    for r in range(TOPK // 8):
                        src = S if r == 0 else R
                        m8 = M[:, h, 8 * r:8 * r + 8]
                        dve.sem_inc(s_here, 1)
                        dve.max(m8, src[:, h, :]).then_inc(*VL.done(f"m{r}{h}"))
                        dve.wait_ge(*VL(f"m{r}{h}", b))
                        if r == 0:
                            dve.wait_ge(*GL(f"d{h}", b - 1))
                        dve.sem_inc(s_here, 1)
                        dve.match_replace(R[:, h, :], m8, src[:, h, :], GONE).then_inc(*VL.done(f"r{r}{h}"))
                        dve.wait_ge(*VL(f"r{r}{h}", b))
                    dve.tensor_scalar(nmx[:, h:h + 1], M[:, h, 0:1], -1.0, None, ALU.mult).then_inc(*VL.done(f"n{h}"))
                for h in heads:
                    dve.wait_ge(*AL(f"z{h}", b))
                    dve.reciprocal(rz[:, h:h + 1], Zs[:, h:h + 1]).then_inc(*VL.done(f"rz{h}"))
                    dve.wait_ge(*VL(f"rz{h}", b))
                    dve.tensor_tensor(rz[:, h:h + 1], rz[:, h:h + 1], tmq[:, bass.ds(b, 1)], ALU.mult).then_inc(*VL.done(f"w{h}"))
                    dve.wait_ge(*VL(f"w{h}", b))
                    dve.wait_ge(*PL("a", b - 1))
                    dve.tensor_scalar(diag[:, h, :], G.ident[0:T, 0:T], rz[:, h:h + 1], None, ALU.mult).then_inc(*VL.done(f"d{h}"))

        @block.scalar
        def _(act):
            norm_scalar(act, "", V, A, mv, rs, G.eps)
            turn_scalar(act, P, A, pt, XT)
            for i in range(2):
                act.wait_ge(*P(f"q{i}"))
                act.activation(QT[:, i * 400:(i + 1) * 400], pk[:, i, 0:400], ACT.Copy,
                               scale=float(DH0 ** -0.5)).then_inc(*A.done(f"q{i}"))
            act.wait_ge(*A("q1"))
            act.sem_inc(AL.sem, len(AL.names))
            with act.Fori(0, B) as b:
                act.wait_ge(*PL(f"s{H0 - 1}", b - 1))
                act.activation(QTb[:], QT[:, bass.ds(b * T, T)], ACT.Copy).then_inc(*AL.done("q"))
                for i in range(2):
                    act.wait_ge(*PL("k", b))
                    act.activation(KT[:, i * 361:(i + 1) * 361], pk[:, i, 0:361], ACT.Copy).then_inc(*AL.done(f"k{i}"))
                for h in heads:
                    act.wait_ge(*PL(f"s{h}", b))
                    act.wait_ge(*PL("a", b - 1))
                    act.activation(S[:, h, :].rearrange("p (i j) -> p i j", i=2), pss[0:T, h % 2, :, 0:361],
                                   ACT.Copy).then_inc(*AL.done(f"s{h}"))
                for h in heads:
                    act.wait_ge(*VL(f"n{h}", b))
                    act.activation(S[:, h, :], S[:, h, :], ACT.Exp, bias=nmx[:, h:h + 1]).then_inc(*AL.done(f"e1{h}"))
                    act.activation(R[:, h, :], R[:, h, :], ACT.Exp, bias=nmx[:, h:h + 1]).then_inc(*AL.done(f"e2{h}"))
                    if h:
                        act.wait_ge(*AL(f"z{h - 1}", b))
                    act.activation(ME[:], M[:, h, :], ACT.Exp, bias=nmx[:, h:h + 1],
                                   accum_out=Zs[:, h:h + 1]).then_inc(*AL.done(f"z{h}"))
                act.wait_ge(*PL("a", b))
                act.activation(AT[:, 0:KJ - 1, :], pt[:, 0, 0:(KJ - 1) * T].rearrange("p (k t) -> p k t", t=T),
                               ACT.Copy).then_inc(*AL.done("a"))
                act.activation(AT[0:JTAIL, KJ - 1, :], pt[0:JTAIL, 1, 0:T], ACT.Copy).then_inc(*AL.done("a5"))
                act.wait_ge(*PL("c", b))
                act.activation(G.cpT[:, :, bass.ds(b * T, T)], pk[:, 0, 0:KC * T].rearrange("p (k t) -> p k t", t=T),
                               ACT.Copy).then_inc(*AL.done("c"))

        @block.tensor
        def _(pe):
            turn_tensor(pe, P, A, lambda b: V(f"centred{b}"), G.N, pt, G.ident)
            pe.wait_ge(s_w, 32)
            pe.wait_ge(*A(f"turned{B - 1}"))
            for i in range(2):
                for k in range(KD):
                    ins = pe.matmul(pk[:, i, 0:400], Wq[:, k, :], XT[:, k, i * 400:(i + 1) * 400],
                                    start=k == 0, stop=k == KD - 1)
                ins.then_inc(*P.done(f"q{i}"))
            pe.wait_ge(*A("q1"))
            pe.sem_inc(PL.sem, len(PL.names))
            with pe.Fori(0, B) as b:
                pe.wait_ge(s_ct, 16 * b + 16)
                pe.wait_ge(*AL("c", b - 1))
                for i in range(2):
                    for k in range(KC):
                        ins = pe.matmul(pk[:, i, 0:361], Wk[:, k, :], CT[:, k, i * 361:(i + 1) * 361],
                                        start=k == 0, stop=k == KC - 1)
                ins.then_inc(*PL.done("k"))
                pe.wait_ge(*AL("k1", b))
                for h in heads:
                    if h >= 2:
                        pe.wait_ge(*AL(f"s{h - 2}", b))
                    for i in range(2):
                        ins = pe.matmul(pss[0:T, h % 2, i, 0:361], QTb[32 * h:32 * h + 32, :],
                                        KT[32 * h:32 * h + 32, i * 361:(i + 1) * 361], start=True, stop=True,
                                        tile_position=(32 * h, 0))
                    ins.then_inc(*PL.done(f"s{h}"))
                pe.wait_ge(*VL(f"d{H0 - 1}", b))
                pe.wait_ge(*GL(f"d{H0 - 1}", b))
                for k in range(KJ):
                    n = 128 if k < KJ - 1 else JTAIL
                    out = pt[0:n, 0, k * T:(k + 1) * T] if k < KJ - 1 else pt[0:n, 1, 0:T]
                    for h in heads:
                        ins = pe.matmul(out, S[:, h, k * 128:k * 128 + n], diag[:, h, :], start=h == 0, stop=h == H0 - 1)
                ins.then_inc(*PL.done("a"))
                pe.wait_ge(*AL("a5", b))
                pe.wait_ge(s_cr, 32 * b + 32)
                for k in range(KC):
                    for j in range(KJ):
                        n = 128 if j < KJ - 1 else JTAIL
                        ins = pe.matmul(pk[:, 0, k * T:(k + 1) * T], CR[0:n, j, k * 128:(k + 1) * 128], AT[0:n, j, :],
                                        start=j == 0, stop=j == KJ - 1)
                ins.then_inc(*PL.done("c"))


def stage_film_conv(nc, I, G):
    with ExitStack() as ctx:
        c = Core(nc, ctx, "film")
        st, mv, rs = c.sb("st", [T, B, 6]), c.sb("mv", [T, B, 2]), c.sb("rs", [T, 2, B])
        gain, shift = c.sb("gain", [T, D]), c.sb("shift", [T, D])
        Wv = c.sb("Wv", [128, KC, D])
        Wf = [c.sb(f"Wf{i}", [128, KD, 2 * D]) for i in range(2)]
        bf = c.sb("bf", [T, 4, D])
        mg = c.sb("mg", [T, 1])
        cT = c.sb("cT", [128, KD, NTOK])
        X1 = c.sb("X1", [T, B, D])
        U = c.sb("U", [T, 2, D])
        F = [c.sb(n, [T, NFREQ]) for n in ("Fc", "Fs")]
        Gm = [c.sb(n, [NFREQ, T]) for n in ("Gc", "Gn", "Gs")]
        PR = c.sb("PR", [NFREQ, 2, 4, D])
        pc = c.ps("pc", [128, 2, 512])
        pf = c.ps("pf", [128, 2, 512])
        px = c.ps("px", [128, 2, 512])
        py = c.ps("py", [128, 2, 512])
        s_w, s_k = c.sem("weights_in"), c.sem("consts_in")
        V = Steps(c.sem("vector"), norm_vec_names("", True)
                  + ["b0", "b1", "b2", "b3", "b4"]
                  + [f"{n}{b}" for b in range(B) for n in ("u", "x", "y", "z")]
                  + [f"{n}{b}" for b in range(B) for n in ("p0", "p1", "p2", "p3", "ou", "ox", "oy", "oz")])
        A = Steps(c.sem("scalar"), ["std"] + [f"c{i}" for i in range(8)])
        P = Steps(c.sem("tensor"), [f"c{i}" for i in range(8)] + [f"f{b}" for b in range(B)]
                  + [f"{n}{b}" for b in range(B) for n in ("d", "o", "i")])
        GP = Steps(c.sem("pool"), [f"r{b}" for b in range(B)])
        block = c.block()

        @block.sync
        def _(sp):
            sp.dma_start(Wv[:], I["L0_Wv"].rearrange("(k p) n -> p k n", p=128)).then_inc(s_w, 16)
            sp.dma_start(Wf[0][:], I["Wf_in"].rearrange("(k p) n -> p k n", p=128)).then_inc(s_w, 16)
            sp.dma_start(Wf[1][:], I["Wf_out"].rearrange("(k p) n -> p k n", p=128)).then_inc(s_w, 16)
            sp.dma_start(gain[:], row_bcast(I["g_in"], T)).then_inc(s_k, 16)
            sp.dma_start(shift[:], row_bcast(I["b_in"], T)).then_inc(s_k, 16)
            sp.dma_start(bf[:, 0:2, :].rearrange("p a d -> p (a d)"), row_bcast(I["bf_in"], T)).then_inc(s_k, 16)
            sp.dma_start(bf[:, 2:4, :].rearrange("p a d -> p (a d)"), row_bcast(I["bf_out"], T)).then_inc(s_k, 16)
            sp.dma_start(mg[:], row_bcast(I["mod_gate"], T)).then_inc(s_k, 16)
            for t, n in zip(F + Gm, ("Fc", "Fs", "Gc", "Gn", "Gs")):
                sp.dma_start(t[:], I[n]).then_inc(s_k, 16)

        @block.gpsimd
        def _(pool):
            pool.wait_ge(*V("b4"))
            for b in range(B):
                pool.tensor_tensor(G.Y[:, b, :], G.N[:, b, :], bf[:, 3, :], ALU.add).then_inc(*GP.done(f"r{b}"))

        @block.vector
        def _(dve):
            tt, ts, stt = dve.tensor_tensor, dve.tensor_scalar, dve.scalar_tensor_tensor
            dve.wait_ge(s_k, 160)
            norm_vector(dve, "", V, A, G.N, X1, st, mv, rs, gain[:], shift[:])
            ts(bf[:, 0, :], bf[:, 0, :], mg[:, 0:1], 1.0, ALU.mult, ALU.add).then_inc(*V.done("b0"))
            ts(bf[:, 1, :], bf[:, 1, :], mg[:, 0:1], None, ALU.mult).then_inc(*V.done("b1"))
            ts(bf[:, 2, :], bf[:, 2, :], mg[:, 0:1], 1.0, ALU.mult, ALU.add).then_inc(*V.done("b2"))
            ts(bf[:, 3, :], bf[:, 3, :], mg[:, 0:1], None, ALU.mult).then_inc(*V.done("b3"))
            dve.wait_ge(*V("b3"))
            dve.tensor_copy(U[:, 0, 0:1], bf[:, 3, 0:1]).then_inc(*V.done("b4"))
            dve.wait_ge(*V("b4"))
            for b in range(B):
                x1 = X1[:, b, :]
                dve.wait_ge(*P(f"f{b}"))
                stt(U[:, 0, :], pf[0:T, 0, :], mg[:, 0:1], bf[:, 0, :], ALU.mult, ALU.add).then_inc(*V.done(f"u{b}"))
                dve.wait_ge(*V(f"u{b}"))
                tt(x1, x1, U[:, 0, :], ALU.mult).then_inc(*V.done(f"x{b}"))
                dve.wait_ge(*V(f"x{b}"))
                stt(x1, pf[0:T, 1, :], mg[:, 0:1], x1, ALU.mult, ALU.add).then_inc(*V.done(f"y{b}"))
                dve.wait_ge(*V(f"y{b}"))
                tt(x1, x1, bf[:, 1, :], ALU.add).then_inc(*V.done(f"z{b}"))
            for b in range(B):
                dve.wait_ge(*P(f"d{b}"))
                if b >= 2:
                    dve.wait_ge(*P(f"i{b - 2}"))
                for i, (u, v) in enumerate(((0, 0), (1, 1), (0, 1), (1, 0))):
                    tt(PR[:, b % 2, i, :], px[0:NFREQ, u, :], G.Kf[:, v, :], ALU.mult).then_inc(*V.done(f"p{i}{b}"))
                dve.wait_ge(*P(f"o{b}"))
                dve.wait_ge(*GP(f"r{b}"))
                if b:
                    dve.wait_ge(*V(f"oy{b - 1}"))
                stt(U[:, 0, :], pf[0:T, 0, :], mg[:, 0:1], bf[:, 2, :], ALU.mult, ALU.add).then_inc(*V.done(f"ou{b}"))
                dve.wait_ge(*V(f"ou{b}"))
                dve.wait_ge(*P(f"i{b}"))
                tt(U[:, 1, :], py[0:T, b % 2, :], U[:, 0, :], ALU.mult).then_inc(*V.done(f"ox{b}"))
                dve.wait_ge(*V(f"ox{b}"))
                stt(U[:, 1, :], pf[0:T, 1, :], mg[:, 0:1], U[:, 1, :], ALU.mult, ALU.add).then_inc(*V.done(f"oy{b}"))
                dve.wait_ge(*V(f"oy{b}"))
                tt(G.Y[:, b, :], G.Y[:, b, :], U[:, 1, :], ALU.add).then_inc(*V.done(f"oz{b}"))

        @block.scalar
        def _(act):
            norm_scalar(act, "", V, A, mv, rs, G.eps)
            for i in range(8):
                act.wait_ge(*P(f"c{i}"))
                act.activation(cT[:, i // 2, (i % 2) * 400:(i % 2 + 1) * 400], pc[:, i % 2, 0:400],
                               ACT.Copy).then_inc(*A.done(f"c{i}"))

        @block.tensor
        def _(pe):
            pe.wait_ge(s_w, 48)
            for i in range(8):
                if i >= 2:
                    pe.wait_ge(*A(f"c{i - 2}"))
                for k in range(KC):
                    ins = pe.matmul(pc[:, i % 2, 0:400], Wv[:, k, (i // 2) * 128:(i // 2 + 1) * 128],
                                    G.cpT[:, k, (i % 2) * 400:(i % 2 + 1) * 400], start=k == 0, stop=k == KC - 1)
                ins.then_inc(*P.done(f"c{i}"))
            pe.wait_ge(*A("c7"))

            def film(w, b):
                for part in range(2):
                    for k in range(KD):
                        ins = pe.matmul(pf[0:T, part, :], cT[:, k, b * T:(b + 1) * T],
                                        Wf[w][:, k, part * D:(part + 1) * D], start=k == 0, stop=k == KD - 1)
                return ins

            for b in range(B):
                if b:
                    pe.wait_ge(*V(f"y{b - 1}"))
                film(0, b).then_inc(*P.done(f"f{b}"))
            pe.wait_ge(*V(f"y{B - 1}"))
            for b in range(B):
                pe.wait_ge(*V(f"z{b}"))
                if b:
                    pe.wait_ge(*V(f"p3{b - 1}"))
                for ch in range(2):
                    ins = pe.matmul(px[0:NFREQ, ch, :], F[ch][:], X1[:, b, :], start=True, stop=True)
                ins.then_inc(*P.done(f"d{b}"))
                if b:
                    pe.wait_ge(*V(f"oy{b - 1}"))
                film(1, b).then_inc(*P.done(f"o{b}"))
                pe.wait_ge(*V(f"p3{b}"))
                for i, g in enumerate((Gm[0], Gm[1], Gm[2], Gm[2])):
                    ins = pe.matmul(py[0:T, b % 2, :], g[:], PR[:, b % 2, i, :], start=i == 0, stop=i == 3)
                ins.then_inc(*P.done(f"i{b}"))


def stage_mlp(nc, I, G):
    with ExitStack() as ctx:
        c = Core(nc, ctx, "mlp")
        st, mv, rs = c.sb("st", [T, B, 6]), c.sb("mv", [T, B, 2]), c.sb("rs", [T, 2, B])
        rows = c.sb("rows", [T, 5, D])
        b1 = c.sb("b1", [128, KF])
        W1, W2 = c.sb("W1", [128, KD, FF]), c.sb("W2", [128, KF, D])
        HT = c.sb("HT", [128, KF, NTOK])
        pt = c.ps("pt", [128, 2, 512])
        ph = c.ps("ph", [128, 4, 512])
        py = c.ps("py", [128, 2, 512])
        s_w1, s_w2, s_k = c.sem("w1_in"), c.sem("w2_in"), c.sem("consts_in")
        NH = 2 * KF
        V = Steps(c.sem("vector"), norm_vec_names("f", True) + [f"{n}{b}" for b in range(B) for n in ("y", "z")]
                  + norm_vec_names("o", True) + [f"x{b}" for b in range(B)])
        A = Steps(c.sem("scalar"), ["fstd"] + turn_names() + [f"h{i}" for i in range(NH)] + ["ostd"])
        P = Steps(c.sem("tensor"), turn_names() + [f"h{i}" for i in range(NH)] + [f"y{b}" for b in range(B)])
        block = c.block()

        @block.sync
        def _(sp):
            for i, n in enumerate(("g_ffn", "b_ffn", "g_out", "b_out", "b2")):
                sp.dma_start(rows[:, i, :], row_bcast(I[n], T)).then_inc(s_k, 16)
            sp.dma_start(b1[:], I["b1"]).then_inc(s_k, 16)
            sp.dma_start(W1[:], I["W1"].rearrange("(k p) n -> p k n", p=128)).then_inc(s_w1, 16)
            sp.dma_start(W2[:], I["W2"].rearrange("(k p) n -> p k n", p=128)).then_inc(s_w2, 16)

        @block.vector
        def _(dve):
            dve.wait_ge(s_k, 96)
            norm_vector(dve, "f", V, A, G.Y, G.N, st, mv, rs, rows[:, 0, :], rows[:, 1, :])
            for b in range(B):
                dve.wait_ge(*P(f"y{b}"))
                dve.tensor_tensor(G.Y[:, b, :], py[0:T, b % 2, :], G.Y[:, b, :], ALU.add).then_inc(*V.done(f"y{b}"))
                dve.wait_ge(*V(f"y{b}"))
                dve.tensor_tensor(G.Y[:, b, :], G.Y[:, b, :], rows[:, 4, :], ALU.add).then_inc(*V.done(f"z{b}"))
            dve.wait_ge(*V(f"z{B - 1}"))
            norm_vector(dve, "o", V, A, G.Y, G.N, st, mv, rs, rows[:, 2, :], rows[:, 3, :])
            for b in range(B):
                dve.wait_ge(*V(f"oshifted{b}"))
                dve.tensor_tensor(G.X[:, b, :], G.X[:, b, :], G.N[:, b, :], ALU.add).then_inc(*V.done(f"x{b}"))

        @block.scalar
        def _(act):
            norm_scalar(act, "f", V, A, mv, rs, G.eps)
            turn_scalar(act, P, A, pt, G.XT)
            for i in range(NH):
                act.wait_ge(*P(f"h{i}"))
                act.activation(HT[:, i // 2, (i % 2) * 400:(i % 2 + 1) * 400], ph[:, i % 4, 0:400], ACT.Gelu,
                               bias=b1[:, i // 2:i // 2 + 1]).then_inc(*A.done(f"h{i}"))
            norm_scalar(act, "o", V, A, mv, rs, G.eps)

        @block.tensor
        def _(pe):
            turn_tensor(pe, P, A, lambda b: V(f"fshifted{b}"), G.N, pt, G.ident)
            pe.wait_ge(*A(f"turned{B - 1}"))
            pe.wait_ge(s_w1, 16)
            for i in range(NH):
                f, half = divmod(i, 2)
                if i >= 4:
                    pe.wait_ge(*A(f"h{i - 4}"))
                for k in range(KD):
                    ins = pe.matmul(ph[:, i % 4, 0:400], W1[:, k, f * 128:(f + 1) * 128],
                                    G.XT[:, k, half * 400:(half + 1) * 400], start=k == 0, stop=k == KD - 1)
                ins.then_inc(*P.done(f"h{i}"))
            pe.wait_ge(*A(f"h{NH - 1}"))
            pe.wait_ge(s_w2, 16)
            for b in range(B):
                if b >= 2:
                    pe.wait_ge(*V(f"y{b - 2}"))
                for f in range(KF):
                    ins = pe.matmul(py[0:T, b % 2, :], HT[:, f, b * T:(b + 1) * T], W2[:, f, :],
                                    start=f == 0, stop=f == KF - 1)
                ins.then_inc(*P.done(f"y{b}"))


def stage_router(nc, I, G, top, wg, bg, cap, xe, first, w1, w2):
    with ExitStack() as ctx:
        c = Core(nc, ctx, f"route{top}")
        st, mv, rs = c.sb("st", [T, B, 6]), c.sb("mv", [T, B, 2]), c.sb("rs", [T, 2, B])
        Wg = c.sb("Wg", [128, KD, E])
        bgr = c.sb("bgr", [T, E])
        iom8 = c.sb("iom8", [T, E])
        tri, ones = c.sb("tri", [T, T]), c.sb("ones", [T, T])
        trash = c.sb("trash", [T, 2, B])
        L, EX, Q1, Q2 = (c.sb(n, [T, B, E]) for n in ("L", "EX", "Q1", "Q2"))
        oh = c.sb("oh", [T, 2, B, E])
        pre = c.sb("pre", [T, 2, B + 1, E])
        mx, idx = c.sb("mx", [T, 2, B]), c.sb("idx", [T, 2, B])
        pos, kp, fs, fg = (c.sb(n, [T, 2, B]) for n in ("pos", "kp", "fs", "fg"))
        sm, t1, t2 = (c.sb(n, [T, B]) for n in ("sm", "t1", "t2"))
        put = c.sb("put", [T, 2, B], I32)
        pt = c.ps("pt", [128, 2, 512])
        pl = c.ps("pl", [T, 512])
        pp = c.ps("pp", [T, 2, 512])
        over, level = c.sb("over", [1, len(WIDTHS) - 1, E]), c.sb("level", [1, E])
        s_k, s_out = c.sem("consts_in"), c.sem("rows_out")
        names = norm_vec_names("", False) + ["logit", "mx0", "sub", "sum"]
        for n in range(top):
            if n:
                names += ["hide", "mx1"]
            names += [f"{x}{n}" for x in ("eq", "c", "idx", "oh")]
        for n in range(top):
            names += [f"pre{n}_{b}" for b in range(B + 1)]
        names += ["all"] if top == 2 else []
        for n in range(top):
            names += [f"{x}{n}" for x in ("cum", "pos", "pos1", "keep", "base", "slot", "tr", "trk", "tra", "put",
                                          "pk", "sg", "get")]
        names += ["g0"] + (["g1d"] if top == 2 else []) + (["g1", "dsum", "den", "rden", "w0", "w1"] if top == 2 else [])
        names += [f"wk{n}" for n in range(top)]
        names += ([f"over{i}" for i in range(len(WIDTHS) - 1)] + ["level", "level_i"]) if top == 2 else []
        V = Steps(c.sem("vector"), names)
        A = Steps(c.sem("scalar"), ["std"] + turn_names() + ["exp"] + (["exp1"] if top == 2 else []))
        P = Steps(c.sem("tensor"), turn_names() + ["logits"] + [f"cum{n}" for n in range(top)] + (["count"] if top == 2 else []))
        block = c.block()
        bb = lambda col: over_d(col, E)

        @block.sync
        def _(sp):
            sp.dma_start(Wg[:], wg.rearrange("(k p) e -> p k e", p=128)).then_inc(s_k, 16)
            sp.dma_start(bgr[:], row_bcast(bg, T)).then_inc(s_k, 16)
            sp.dma_start(iom8[:], row_bcast(I["iota_m8"], T)).then_inc(s_k, 16)
            sp.dma_start(tri[:], I["tri"]).then_inc(s_k, 16)
            sp.dma_start(ones[:], I["ones"]).then_inc(s_k, 16)
            sp.dma_start(trash[:], I[f"trash{top}"]).then_inc(s_k, 16)
            sp.dma_start(first.W1[:], w1[0].rearrange("(k p) f -> p k f", p=128)).then_inc(first.s_w1, 16)
            sp.dma_start(first.W2[:], w2[0].rearrange("(k p) f -> p k f", p=128)).then_inc(first.s_w2, 16)

        @block.gpsimd
        def _(pool):
            for n in range(top):
                pool.wait_ge(*V(f"put{n}"))
                for b in range(B):
                    pool.indirect_dma_start(xe[:, :], bass.IndirectOffsetOnAxis(ap=put[:, n, b:b + 1], axis=0),
                                            G.N[:, b, :], None).then_inc(s_out, 16)
            pool.wait_ge(s_out, 16 * top * B)

        @block.vector
        def _(dve):
            tt, ts, stt = dve.tensor_tensor, dve.tensor_scalar, dve.scalar_tensor_tensor

            def step(ins, name):
                ins.then_inc(*V.done(name))
                dve.wait_ge(*V(name))

            norm_vector(dve, "", V, A, G.X, G.N, st, mv, rs)
            dve.wait_ge(s_k, 96)
            dve.wait_ge(*P("logits"))
            step(tt(L[:], pl[:, 0:B * E].rearrange("p (b e) -> p b e", e=E), over_b(bgr[:]), ALU.add), "logit")
            step(dve.tensor_reduce(mx[:, 0], L[:], AX.X, ALU.max), "mx0")
            step(tt(EX[:], L[:], bb(mx[:, 0]), ALU.subtract), "sub")
            dve.wait_ge(*A("exp"))
            step(dve.tensor_reduce(sm[:], EX[:], AX.X, ALU.add), "sum")
            for n in range(top):
                if n:
                    step(stt(Q2[:].rearrange("p b e -> p (b e)"), oh[:, 0].rearrange("p b e -> p (b e)"), FLOOR,
                             L[:].rearrange("p b e -> p (b e)"), ALU.mult, ALU.add), "hide")
                    step(dve.tensor_reduce(mx[:, 1], Q2[:], AX.X, ALU.max), "mx1")
                src = Q2 if n else L
                step(tt(Q1[:], src[:], bb(mx[:, n]), ALU.is_ge), f"eq{n}")
                step(tt(Q1[:], Q1[:], over_b(iom8[:]), ALU.mult), f"c{n}")
                step(dve.tensor_reduce(idx[:, n], Q1[:], AX.X, ALU.min), f"idx{n}")
                step(tt(oh[:, n], over_b(iom8[:]), bb(idx[:, n]), ALU.is_equal), f"oh{n}")
            for n in range(top):
                for b in range(B + 1):
                    if b == 0:
                        step(ts(pre[:, n, 0, :], oh[:, n, 0, :], 0.0, None, ALU.mult), f"pre{n}_0")
                    else:
                        step(tt(pre[:, n, b, :], pre[:, n, b - 1, :], oh[:, n, b - 1, :], ALU.add), f"pre{n}_{b}")
            if top == 2:
                step(tt(pre[:, 1, 0:B, :], pre[:, 1, 0:B, :], over_b(pre[:, 0, B, :]), ALU.add), "all")
            for n in range(top):
                dve.wait_ge(*P(f"cum{n}"))
                step(tt(Q1[:], pp[:, n, 0:B * E].rearrange("p (b e) -> p b e", e=E), oh[:, n], ALU.mult), f"cum{n}")
                step(dve.tensor_reduce(pos[:, n], Q1[:], AX.X, ALU.add), f"pos{n}")
                step(ts(pos[:, n], pos[:, n], -1.0, None, ALU.add), f"pos1{n}")
                step(ts(kp[:, n], pos[:, n], float(cap), None, ALU.is_lt), f"keep{n}")
                step(ts(fg[:, n], idx[:, n], 8.0, float(cap), ALU.add, ALU.mult), f"base{n}")
                step(tt(fs[:, n], fg[:, n], pos[:, n], ALU.add), f"slot{n}")
                step(tt(fs[:, n], fs[:, n], trash[:, n], ALU.subtract), f"tr{n}")
                step(tt(fs[:, n], fs[:, n], kp[:, n], ALU.mult), f"trk{n}")
                step(tt(fs[:, n], fs[:, n], trash[:, n], ALU.add), f"tra{n}")
                step(dve.tensor_copy(put[:, n], fs[:, n]), f"put{n}")
                step(tt(pos[:, n], pos[:, n], kp[:, n], ALU.mult), f"pk{n}")
                step(tt(fg[:, n], fg[:, n], pos[:, n], ALU.add), f"sg{n}")
                step(dve.tensor_copy(G.slot[:, n], fg[:, n]), f"get{n}")
            step(dve.reciprocal(G.wt[:, 0], sm[:]), "g0")
            if top == 2:
                step(tt(t1[:], mx[:, 1], mx[:, 0], ALU.subtract), "g1d")
                dve.wait_ge(*A("exp1"))
                step(tt(G.wt[:, 1], t2[:], G.wt[:, 0], ALU.mult), "g1")
                step(tt(t1[:], G.wt[:, 0], G.wt[:, 1], ALU.add), "dsum")
                step(ts(t1[:], t1[:], 1e-9, None, ALU.add), "den")
                step(dve.reciprocal(t1[:], t1[:]), "rden")
                step(tt(G.wt[:, 0], G.wt[:, 0], t1[:], ALU.mult), "w0")
                step(tt(G.wt[:, 1], G.wt[:, 1], t1[:], ALU.mult), "w1")
            for n in range(top):
                step(tt(G.wt[:, n], G.wt[:, n], kp[:, n], ALU.mult), f"wk{n}")
            if top == 2:
                dve.wait_ge(*P("count"))
                for i, w in enumerate(WIDTHS[:-1]):
                    step(ts(over[:, i, :], pp[0:1, 0, 128:128 + E], w + 0.5, None, ALU.is_ge), f"over{i}")
                step(dve.tensor_reduce(level[:], over[:].rearrange("p i e -> p e i"), AX.X, ALU.add), "level")
                step(dve.tensor_copy(G.level[:], level[:]), "level_i")

        @block.scalar
        def _(act):
            norm_scalar(act, "", V, A, mv, rs, G.eps)
            turn_scalar(act, P, A, pt, G.XT)
            act.wait_ge(*V("sub"))
            act.activation(EX[:], EX[:], ACT.Exp).then_inc(*A.done("exp"))
            if top == 2:
                act.wait_ge(*V("g1d"))
                act.activation(t2[:], t1[:], ACT.Exp).then_inc(*A.done("exp1"))

        @block.tensor
        def _(pe):
            turn_tensor(pe, P, A, lambda b: V(f"centred{b}"), G.N, pt, G.ident)
            pe.wait_ge(s_k, 96)
            pe.wait_ge(*A(f"turned{B - 1}"))
            for b in range(B):
                for k in range(KD):
                    ins = pe.matmul(pl[:, b * E:(b + 1) * E], G.XT[:, k, b * T:(b + 1) * T], Wg[:, k, :],
                                    start=k == 0, stop=k == KD - 1)
            ins.then_inc(*P.done("logits"))
            for n in range(top):
                pe.wait_ge(*V("all" if top == 2 else f"pre{n}_{B}"))
                flat = lambda a: a.rearrange("p b e -> p (b e)")
                pe.matmul(pp[:, n, 0:B * E], tri[:], flat(oh[:, n]), start=True, stop=False)
                pe.matmul(pp[:, n, 0:B * E], ones[:], flat(pre[:, n, 0:B, :]), start=False,
                          stop=True).then_inc(*P.done(f"cum{n}"))
            if top == 2:
                pe.wait_ge(*V("cum0"))
                for n in range(top):
                    ins = pe.matmul(pp[0:1, 0, 128:128 + E], ones[:, 0:1], pre[:, n, B, :], start=n == 0, stop=n == top - 1)
                ins.then_inc(*P.done("count"))


class FirstWeights:

    def __init__(self, c):
        self.W1, self.W2 = c.sb("W1", [128, KD, FF]), c.sb("W2", [128, KF, D])
        self.s_w1, self.s_w2 = c.sem("w1_in"), c.sem("w2_in")


def stage_experts(nc, I, G, top, func, w1, b1, w2, b2, cap, xe, ye, first, widths):
    rows_of = [min(128, cap - o) for o in range(0, cap, 128)]
    NT, R = len(rows_of), rows_of[0]
    whole = NT if rows_of[-1] == R else NT - 1
    NX = 16 if whole == NT else 32
    tiles = lambda w: range((w + 127) // 128)
    with ExitStack() as ctx:
        c = Core(nc, ctx, f"ffn{top}")
        W1, W2, s_w1, s_w2 = first.W1, first.W2, first.s_w1, first.s_w2
        b1c = c.sb("b1c", [128, E, KF])
        b1e = c.sb("b1e", [128, KF])
        b2r = c.sb("b2r", [R, D])
        XE = c.sb("XE", [R, NT, D])
        XET = c.sb("XET", [128, KD, cap])
        HT = c.sb("HT", [128, KF, cap])
        Y = c.sb("Y", [R, NT, D])
        got = G.Y
        pt = c.ps("pt", [128, 2, 512])
        ph = c.ps("ph", [128, 4, 512])
        py = c.ps("py", [128, 2, 512])
        s_b1, s_b2, s_x, s_y = (c.sem(n) for n in ("b1_in", "b2_in", "rows_in", "rows_out"))
        s_g = [c.sem(f"gathered{b}") for b in range(B)]
        s_free = c.sem("results_free")
        P = Steps(c.sem("tensor"), [f"t{k}" for k in range(KD)] + [f"h{f}" for f in range(KF)]
                  + [f"y{n}" for n in range(NT)], ahead=1)
        A = Steps(c.sem("scalar"), ["b1"] + [f"t{k}" for k in range(KD)] + [f"h{f}" for f in range(KF)], ahead=1)
        V = Steps(c.sem("vector"), [f"y{n}" for n in range(NT)], ahead=1)
        GP = Steps(c.sem("pool"), ["ht0"])
        VG = Steps(c.sem("combined"), [f"x{n}_{b}" for n in range(top) for b in range(B)])
        block = c.block()

        def by_width(eng, e, S, body):
            if len(widths) == 1:
                body(widths[0])
                return
            level = eng.value_load(G.level[0:1, bass.ds(e, 1)], min_val=0, max_val=len(widths) - 1)
            start = S.next
            for i, w in enumerate(widths):
                S.next = start
                with eng.If(level == i):
                    body(w)

        @block.sync
        def _(sp):
            xe_v = xe[0:E * cap, :].rearrange("(e r) d -> e r d", e=E)

            def load_rows(e):
                one = xe_v[e].rearrange("o r d -> (o r) d")
                sp.dma_start(XE[:, 0:whole, :], one[0:R * whole, :].rearrange("(n r) d -> r n d", n=whole)).then_inc(s_x, 16)
                if whole < NT:
                    sp.dma_start(XE[0:rows_of[-1], whole, :], one[R * whole:cap, :]).then_inc(s_x, 16)

            sp.dma_start(b1c[:], b1).then_inc(s_b1, 16)
            load_rows(slice(0, 1))
            sp.dma_start(b2r[:], b2[0:1, :].to_broadcast((R, D))).then_inc(s_b2, 16)
            with sp.Fori(0, E - 1) as e:
                one = bass.ds(e + 1, 1)
                sp.wait_ge(*P(f"t{KD - 1}", e))
                load_rows(one)
                sp.wait_ge(*P(f"h{KF - 1}", e))
                sp.dma_start(W1[:], w1[one].rearrange("o (k p) f -> p (o k) f", p=128)).then_inc(s_w1, 16)
                sp.wait_ge(*P(f"y{NT - 1}", e))
                sp.dma_start(W2[:], w2[one].rearrange("o (k p) f -> p (o k) f", p=128)).then_inc(s_w2, 16)
                sp.wait_ge(*V(f"y{NT - 1}", e))
                sp.dma_start(b2r[:], b2[one, :].to_broadcast((R, D))).then_inc(s_b2, 16)

        @block.vector
        def _(dve):
            dve.sem_inc(V.sem, len(V.names))
            with dve.Fori(0, E) as e:
                dve.wait_ge(s_free, e + 1)
                dve.wait_ge(s_b2, 16 * e + 16)

                def add_bias(w):
                    for n in range(NT):
                        dve.wait_ge(*P(f"y{n}", e))
                        r = rows_of[n]
                        if n in tiles(w):
                            dve.tensor_tensor(Y[0:r, n, :], py[0:r, n % 2, :], b2r[0:r, :], ALU.add).then_inc(*V.done(f"y{n}"))
                        else:
                            dve.wait_ge(*V(f"y{n - 1}", e))
                            dve.sem_inc(*V.done(f"y{n}"))

                by_width(dve, e, V, add_bias)
            for n in range(top):
                for b in range(B):
                    dve.wait_ge(s_g[b], 16 * (n + 1))
                    if n:
                        dve.wait_ge(*VG(f"x{n - 1}_{b}"))
                    dve.scalar_tensor_tensor(G.X[:, b, :], got[:, b, :], G.wt[:, n, b:b + 1], G.X[:, b, :],
                                             ALU.mult, ALU.add).then_inc(*VG.done(f"x{n}_{b}"))

        @block.scalar
        def _(act):
            act.sem_inc(A.sem, len(A.names))
            act.wait_ge(s_b1, 16)
            act.wait_ge(*GP("ht0"))
            with act.Fori(0, E) as e:
                act.wait_ge(*A(f"h{KF - 1}", e - 1))
                act.activation(b1e[:], b1c[:, bass.ds(e, 1), :].rearrange("p o f -> p (o f)"), ACT.Copy).then_inc(*A.done("b1"))

                def columns(w):
                    for k in range(KD):
                        act.wait_ge(*P(f"t{k}", e))
                        act.activation(XET[:, k, 0:w], pt[:, k % 2, 0:w], ACT.Copy).then_inc(*A.done(f"t{k}"))
                    act.wait_ge(*A("b1", e))
                    act.wait_ge(*P(f"y{NT - 1}", e - 1))
                    for f in range(KF):
                        act.wait_ge(*P(f"h{f}", e))
                        act.activation(HT[:, f, 0:w], ph[:, f % 4, 0:w], func, bias=b1e[:, f:f + 1]).then_inc(*A.done(f"h{f}"))

                by_width(act, e, A, columns)

        @block.tensor
        def _(pe):
            pe.sem_inc(P.sem, len(P.names))
            with pe.Fori(0, E) as e:
                pe.wait_ge(s_x, NX * e + NX)

                def products(w):
                    for k in range(KD):
                        if k >= 2:
                            pe.wait_ge(*A(f"t{k - 2}", e))
                        for n in tiles(w):
                            r = min(128, w - 128 * n)
                            ins = pe.transpose(pt[:, k % 2, n * 128:n * 128 + r], XE[0:r, n, k * 128:(k + 1) * 128],
                                               G.ident[0:r, 0:r])
                        ins.then_inc(*P.done(f"t{k}"))
                    pe.wait_ge(*A(f"t{KD - 1}", e))
                    pe.wait_ge(s_w1, 16 * e + 16)
                    for f in range(KF):
                        if f >= 4:
                            pe.wait_ge(*A(f"h{f - 4}", e))
                        for k in range(KD):
                            ins = pe.matmul(ph[:, f % 4, 0:w], W1[:, k, f * 128:(f + 1) * 128], XET[:, k, 0:w],
                                            start=k == 0, stop=k == KD - 1)
                        ins.then_inc(*P.done(f"h{f}"))
                    pe.wait_ge(s_w2, 16 * e + 16)
                    pe.wait_ge(*A(f"h{KF - 1}", e))
                    for n in range(NT):
                        if n not in tiles(w):
                            pe.wait_ge(*P(f"y{n - 1}", e))
                            pe.sem_inc(*P.done(f"y{n}"))
                            continue
                        if n >= 2:
                            pe.wait_ge(*V(f"y{n - 2}", e))
                        else:
                            pe.wait_ge(*V(f"y{NT - 1}", e - 1))
                        for f in range(KF):
                            ins = pe.matmul(py[0:rows_of[n], n % 2, :], HT[:, f, n * 128:n * 128 + rows_of[n]], W2[:, f, :],
                                            start=f == 0, stop=f == KF - 1)
                        ins.then_inc(*P.done(f"y{n}"))

                by_width(pe, e, P, products)

        @block.gpsimd
        def _(pool):
            pool.memset(Y[:], 0.0).then_inc(s_free, 1)
            pool.memset(HT[:], 0.0).then_inc(*GP.done("ht0"))
            ye_v = ye.rearrange("(e r) d -> e r d", e=E)
            with pool.Fori(0, E) as e:
                pool.wait_ge(*V(f"y{NT - 1}", e))
                one = ye_v[bass.ds(e, 1)].rearrange("o r d -> (o r) d")
                pool.dma_start(one[0:R * whole, :].rearrange("(n r) d -> r n d", n=whole), Y[:, 0:whole, :]).then_inc(s_y, 16)
                if whole < NT:
                    pool.dma_start(one[R * whole:cap, :], Y[0:rows_of[-1], whole, :]).then_inc(s_y, 16)
                pool.wait_ge(s_y, NX * e + NX)
                pool.sem_inc(s_free, 1)
            for n in range(top):
                for b in range(B):
                    if n:
                        pool.wait_ge(*VG(f"x{n - 1}_{b}"))
                    pool.indirect_dma_start(got[:, b, :], None, ye[:, :],
                                            bass.IndirectOffsetOnAxis(ap=G.slot[:, n, b:b + 1], axis=0)).then_inc(s_g[b], 16)


def stage_latents(nc, I, G):
    with ExitStack() as ctx:
        c = Core(nc, ctx, "lat")
        st, mv, rs = c.sb("st", [T, B, 6]), c.sb("mv", [T, B, 2]), c.sb("rs", [T, 2, B])
        rows = c.sb("rows", [T, 2, D])
        Wq, Wl = c.sb("Wq", [128, KD, D]), c.sb("Wl", [128, KD, 2 * D])
        gam = c.sb("gam", [128, 3])
        SQ = c.sb("SQ", [T, 2, D])
        QK = c.sb("QK", [T, 2, D])
        ss = c.sb("ss", [T, 2, 3, H1])
        pt = c.ps("pt", [128, 2, 512])
        pq = c.ps("pq", [128, 3, 512])
        s_w, s_k = c.sem("weights_in"), c.sem("consts_in")
        V = Steps(c.sem("vector"), norm_vec_names("x", False) + norm_vec_names("l", True) + ["gg", "gs"]
                  + [f"{n}{i}_{b}" for b in range(B) for i in range(2) for n in ("ss", "fl", "rn", "n")])
        A = Steps(c.sem("scalar"), ["xstd", "lstd"] + turn_names()
                  + [f"{n}_{b}" for b in range(B) for n in ("sq0", "sq1", "nm0", "nm1", "v", "t0", "t1")])
        P = Steps(c.sem("tensor"), turn_names() + [f"{n}_{b}" for b in range(B) for n in ("q", "k", "v", "t0", "t1")])
        block = c.block()

        @block.sync
        def _(sp):
            sp.dma_start(rows[:, 0, :], row_bcast(I["ln_l_g"], T)).then_inc(s_k, 16)
            sp.dma_start(rows[:, 1, :], row_bcast(I["ln_l_b"], T)).then_inc(s_k, 16)
            for i, n in enumerate(("qn_g", "kn_g")):
                for h in range(2):
                    sp.dma_start(gam[64 * h:64 * h + 64, i:i + 1], I[n]).then_inc(s_k, 16)
            sp.dma_start(Wq[:], I["WqT"].rearrange("(k p) n -> p k n", p=128)).then_inc(s_w, 16)
            sp.dma_start(Wl[:], I["WlkvT"].rearrange("(k p) n -> p k n", p=128)).then_inc(s_w, 16)

        @block.vector
        def _(dve):
            norm_vector(dve, "x", V, A, G.X, G.N, st, mv, rs)
            dve.wait_ge(*V(f"xcentred{B - 1}"))
            dve.wait_ge(s_k, 96)
            norm_vector(dve, "l", V, A, G.N, G.Y, st, mv, rs, rows[:, 0, :], rows[:, 1, :])
            dve.tensor_tensor(gam[:, 2:3], gam[:, 0:1], gam[:, 1:2], ALU.mult).then_inc(*V.done("gg"))
            dve.wait_ge(*V("gg"))
            dve.tensor_scalar(gam[:, 2:3], gam[:, 2:3], float(DH1 ** -0.5), None, ALU.mult).then_inc(*V.done("gs"))
            for b in range(B):
                for i in range(2):
                    dve.wait_ge(*A(f"sq{i}_{b}"))
                    dve.tensor_reduce(ss[:, i, 0], SQ[:, i, :].rearrange("p (h d) -> p h d", h=H1), AX.X,
                                      ALU.add).then_inc(*V.done(f"ss{i}_{b}"))
                    dve.wait_ge(*V(f"ss{i}_{b}"))
                    dve.tensor_scalar(ss[:, i, 1], ss[:, i, 0], 1.0 / DH1, 1e-16, ALU.mult, ALU.max).then_inc(*V.done(f"fl{i}_{b}"))
                    dve.wait_ge(*A(f"nm{i}_{b}"))
                    dve.reciprocal(ss[:, i, 0], ss[:, i, 2]).then_inc(*V.done(f"rn{i}_{b}"))
                    dve.wait_ge(*V(f"rn{i}_{b}"))
                    if b:
                        dve.wait_ge(*P(f"t{i}_{b - 1}"))
                    dve.tensor_tensor(QK[:, i, :].rearrange("p (h d) -> p h d", h=H1),
                                      pq[0:T, i, :].rearrange("p (h d) -> p h d", h=H1), over_d(ss[:, i, 0], DH1),
                                      ALU.mult).then_inc(*V.done(f"n{i}_{b}"))

        @block.scalar
        def _(act):
            norm_scalar(act, "x", V, A, mv, rs, G.eps)
            norm_scalar(act, "l", V, A, mv, rs, G.eps)
            turn_scalar(act, P, A, pt, G.XT)
            act.wait_ge(*V("gs"))
            for b in range(B):
                for i, n in enumerate("qk"):
                    act.wait_ge(*P(f"{n}_{b}"))
                    if b:
                        act.wait_ge(*V(f"ss{i}_{b - 1}"))
                    act.activation(SQ[:, i, :], pq[0:T, i, :], ACT.Square).then_inc(*A.done(f"sq{i}_{b}"))
                for i in range(2):
                    act.wait_ge(*V(f"fl{i}_{b}"))
                    act.activation(ss[:, i, 2], ss[:, i, 1], ACT.Sqrt).then_inc(*A.done(f"nm{i}_{b}"))
                act.wait_ge(*P(f"v_{b}"))
                act.activation(G.VL[:, b, :], pq[0:T, 2, :], ACT.Copy).then_inc(*A.done(f"v_{b}"))
                for i, dst in enumerate((G.QL, G.KL)):
                    act.wait_ge(*P(f"t{i}_{b}"))
                    out = dst[:, :, b * T:(b + 1) * T]
                    src = pt[:, i, 0:KD * T].rearrange("p (k t) -> p k t", k=KD)
                    if i == 0:
                        ins = act.activation(out, src, ACT.Copy, scale=gam[:, 2:3])
                    else:
                        ins = act.activation(out, src, ACT.Copy)
                    ins.then_inc(*A.done(f"t{i}_{b}"))

        @block.tensor
        def _(pe):
            turn_tensor(pe, P, A, lambda b: V(f"lshifted{b}"), G.Y, pt, G.ident)
            pe.wait_ge(s_w, 32)
            pe.wait_ge(*A(f"turned{B - 1}"))
            for b in range(B):
                for i, (n, w, o) in enumerate((("q", Wq, 0), ("k", Wl, 0), ("v", Wl, D))):
                    if b:
                        pe.wait_ge(*(V(f"n{i}_{b - 1}") if i < 2 else A(f"v_{b - 1}")))
                    for k in range(KD):
                        ins = pe.matmul(pq[0:T, i, :], G.XT[:, k, b * T:(b + 1) * T], w[:, k, o:o + D],
                                        start=k == 0, stop=k == KD - 1)
                    ins.then_inc(*P.done(f"{n}_{b}"))
                for i in range(2):
                    pe.wait_ge(*V(f"n{i}_{b}"))
                    if b:
                        pe.wait_ge(*A(f"t{i}_{b - 1}"))
                    for k in range(KD):
                        ins = pe.transpose(pt[:, i, k * T:(k + 1) * T], QK[:, i, k * 128:(k + 1) * 128], G.ident[0:T, 0:T])
                    ins.then_inc(*P.done(f"t{i}_{b}"))


def stage_attention(nc, I, G, name, J0, near):
    J = JCTX - J0
    KJ = (J + 127) // 128
    JTAIL = J - 128 * (KJ - 1)
    JA = J + T
    NP = (JA + 511) // 512
    PJ, HJ = J // NP, JA // NP
    with ExitStack() as ctx:
        c = Core(nc, ctx, name)
        mine = lambda eng: eng.If(eng.value_load(G.far[0:1, 0:1], min_val=0, max_val=255) == 0 if near else
                                  eng.value_load(G.far[0:1, 0:1], min_val=0, max_val=255) != 0)
        pieces = lambda ap: ap.rearrange("p (i j) -> p i j", i=NP)
        CR = c.sb("CR", [128, KJ, DC])
        CN = c.sb("CN", [128, KJ, DC])
        CT = c.sb("CT", [128, KC, KJ * 128])
        st, mv, rs = c.sb("st", [128, KJ, 6]), c.sb("mv", [128, KJ, 2]), c.sb("rs", [128, 2, KJ])
        gx = c.sb("gx", [128, 2, KC])
        Wkv, Wo = c.sb("Wkv", [128, KC, 2 * D]), c.sb("Wo", [128, KD, D])
        bo = c.sb("bo", [T, D])
        pair = c.sb("pair", [128, 128])
        QTb = c.sb("QTb", [128, KD, T])
        KT = c.sb("KT", [128, KD, JA])
        KS, NM = c.sb("KS", [128, J]), c.sb("NM", [128, J])
        Vv = c.sb("Vv", [128, KJ + 1, D])
        mask8, maskf = c.sb("mask8", [T, J], U8), c.sb("maskf", [T, JA])
        S, Pr = (G.N[:].rearrange("p b d -> p (b d)")[:, o:o + 2 * JA].rearrange("p (i j) -> p i j", i=2)
                 for o in (0, 2048))
        PT = c.sb("PT", [128, 2, KJ + 1, T])
        mx, nmx, Zs, rz = c.sb("mx", [T, H1]), c.sb("nmx", [T, H1]), c.sb("Zs", [T, H1]), c.sb("rz", [T, H1])
        O, OT, XB = c.sb("O", [T, D]), c.sb("OT", [128, KD, T]), c.sb("XB", [T, D])
        pa = c.ps("pa", [128, 2, 512])
        pb = c.ps("pb", [128, 2, 512])
        psc = c.ps("psc", [128, 2, 512])
        po = c.ps("po", [128, 512])
        pv = c.ps("pv", [128, 512])
        s_w, s_cr, s_m = c.sem("weights_in"), c.sem("ctx_in"), c.sem("mask_in")
        s_here = c.sem("waits_met")
        NCR = 16 if JTAIL == 128 else 32
        at = lambda j: (j // 5, slice((j % 5) * T, (j % 5 + 1) * T))
        whole = KJ if JTAIL == 128 else KJ - 1
        tiles = [(j * 128, 128) for j in range(KJ - 1)] + [((KJ - 1) * 128, JTAIL), (J, T)]
        NG = (KJ + 3) // 4
        turns = [(k, g) for k in range(KC) for g in range(NG)]
        g_of = lambda g: (4 * g, min(4 * g + 4, KJ))
        heads = range(H1)
        score_bank = lambda h: psc[0:T, :, 0:HJ] if NP == 2 else psc[0:T, h % 2:h % 2 + 1, 0:HJ]
        V0 = Steps(c.sem("vector_start"), ["tail", "lm"])
        order = [f"x{k}{g}" for k, g in turns] + [f"v{j}" for j in range(KJ)]
        order += [f"{n}{p}" for p in range(KD) for n in ("k", "ss")] + ["s0"]
        for h in heads:
            order += ([f"s{h + 1}"] if h + 1 < H1 else []) + [f"t{h}", f"o{h}"]
        P = Steps(c.sem("tensor"), order + ["ot", "y"], ahead=1)
        A = Steps(c.sem("scalar"), ["q", "std"] + [f"x{k}{g}" for k, g in turns] + [f"v{j}" for j in range(KJ)]
                  + [f"{n}{p}" for p in range(KD) for n in ("sq", "nm")]
                  + [f"{n}{h}" for h in heads for n in (("e", "ta", "tb", "tc") if whole < KJ else ("e", "ta", "tc"))] + ["ot"], ahead=1)
        V = Steps(c.sem("vector"), [f"st{j}" for j in range(KJ)] + [f"mv{j}" for j in range(KJ)] + ["rs"]
                  + [f"c{j}" for j in range(KJ)] + ["mf", "mb"]
                  + [f"{n}{p}" for p in range(KD) for n in ("fl", "rn", "kt")]
                  + [f"{n}{h}" for h in heads for n in ("s", "n")] + ["rz", "o", "y", "yb"], ahead=1)
        GP = Steps(c.sem("pool"), ["kl", "vl"], ahead=1)
        block = c.block()

        @block.sync
        def _(sp):
            sp.dma_start(Wkv[:], I["WkvT"].rearrange("(k p) n -> p k n", p=128)).then_inc(s_w, 16)
            sp.dma_start(Wo[:], I["WoT"].rearrange("(k p) n -> p k n", p=128)).then_inc(s_w, 16)
            sp.dma_start(bo[:], row_bcast(I["bo"], T)).then_inc(s_w, 16)
            sp.dma_start(pair[:], I["pair"]).then_inc(s_w, 16)
            sp.dma_start(gx[:], I["ln_x"]).then_inc(s_w, 16)
            sp.wait_ge(*V0("tail"))
            with mine(sp):
                with sp.Fori(0, B) as b:
                    sp.wait_ge(*V(f"c{KJ - 1}", b - 1))
                    rows = I["ctx"][bass.ds(b, 1), J0:JCTX, :].rearrange("o j c -> (o j) c")
                    sp.dma_start(CR[:, 0:whole, :], rows[0:128 * whole, :].rearrange("(k p) c -> p k c", p=128)).then_inc(s_cr, 16)
                    if whole < KJ:
                        sp.dma_start(CR[0:JTAIL, KJ - 1, :], rows[128 * (KJ - 1):J, :]).then_inc(s_cr, 16)
                    sp.wait_ge(*V("mf", b - 1))
                    sp.sem_inc(s_here, 1)
                    sp.dma_start(mask8[:], I["kmask"][bass.ds(b, 1), J0:JCTX].to_broadcast((T, J))).then_inc(s_m, 16)

        @block.gpsimd
        def _(pool):
            with mine(pool):
                pool.sem_inc(GP.sem, 2)
                with pool.Fori(0, B) as b:
                    pool.wait_ge(*P(f"s{H1 - 1}", b - 1))
                    pool.tensor_copy(KT[:, :, J:JA], G.KL[:, :, bass.ds(b * T, T)]).then_inc(*GP.done("kl"))
                    pool.wait_ge(*P(f"o{H1 - 1}", b - 1))
                    pool.tensor_copy(Vv[0:T, KJ, :], G.VL[:, bass.ds(b, 1), :].rearrange("p o d -> p (o d)")).then_inc(*GP.done("vl"))

        @block.vector
        def _(dve):
            dve.memset(CR[64:128, KJ - 1, :], 0.0).then_inc(*V0.done("tail"))
            dve.memset(maskf[:, J:JA], 0.0).then_inc(*V0.done("lm"))
            with mine(dve):
                dve.sem_inc(V.sem, len(V.names))
                with dve.Fori(0, B) as b:
                    dve.wait_ge(s_cr, NCR * b + NCR)
                    for j in range(KJ):
                        dve.bn_stats(st[:, j, :], CR[:, j, :]).then_inc(*V.done(f"st{j}"))
                    for j in range(KJ):
                        dve.wait_ge(*V(f"st{j}", b))
                        dve.sem_inc(s_here, 1)
                        dve.bn_aggr(mv[:, j, :], st[:, j, :]).then_inc(*V.done(f"mv{j}"))
                    dve.wait_ge(*A("std", b))
                    dve.reciprocal(rs[:, 1, :], rs[:, 0, :]).then_inc(*V.done("rs"))
                    dve.wait_ge(*V("rs", b))
                    dve.wait_ge(*P(f"x{KC - 1}{NG - 1}", b - 1))
                    for j in range(KJ):
                        dve.tensor_scalar(CN[:, j, :], CR[:, j, :], mv[:, j, 0:1], rs[:, 1, j:j + 1], ALU.subtract,
                                          ALU.mult).then_inc(*V.done(f"c{j}"))
                    dve.wait_ge(s_m, 16 * b + 16)
                    dve.tensor_copy(maskf[:, 0:J], mask8[:]).then_inc(*V.done("mf"))
                    dve.wait_ge(*V("mf", b))
                    dve.tensor_scalar(maskf[:, 0:J], maskf[:, 0:J], -1.0, -FLOOR, ALU.add, ALU.mult).then_inc(*V.done("mb"))
                    for p in range(KD):
                        dve.wait_ge(*P(f"ss{p}", b))
                        nm = pieces(NM[:])
                        dve.tensor_scalar(nm, pb[:, 0:NP, 0:PJ], 1.0 / DH1, 1e-16, ALU.mult, ALU.max).then_inc(*V.done(f"fl{p}"))
                        dve.wait_ge(*A(f"nm{p}", b))
                        dve.reciprocal(NM[:], NM[:]).then_inc(*V.done(f"rn{p}"))
                        dve.wait_ge(*V(f"rn{p}", b))
                        dve.tensor_tensor(pieces(KT[:, p, 0:J]), pa[:, 0:NP, 0:PJ], nm,
                                          ALU.mult).then_inc(*V.done(f"kt{p}"))
                    for h in heads:
                        dve.wait_ge(*P(f"s{h}", b))
                        if h >= 2:
                            dve.wait_ge(*A(f"e{h - 2}", b))
                        dve.sem_inc(s_here, 1)
                        dve.tensor_tensor_reduce(pieces(S[:, h % 2, :]), score_bank(h), pieces(maskf[:]), 1.0, GONE, ALU.add, ALU.max,
                                                 mx[:, h:h + 1]).then_inc(*V.done(f"s{h}"))
                        dve.wait_ge(*V(f"s{h}", b))
                        dve.tensor_scalar(nmx[:, h:h + 1], mx[:, h:h + 1], -1.0, None, ALU.mult).then_inc(*V.done(f"n{h}"))
                    dve.wait_ge(*A(f"e{H1 - 1}", b))
                    dve.reciprocal(rz[:], Zs[:]).then_inc(*V.done("rz"))
                    dve.wait_ge(*V("rz", b))
                    dve.wait_ge(*P(f"o{H1 - 1}", b))
                    dve.tensor_tensor(O[:].rearrange("p (h d) -> p h d", h=H1), po[0:T, :].rearrange("p (h d) -> p h d", h=H1),
                                      over_d(rz[:], DH1), ALU.mult).then_inc(*V.done("o"))
                    dve.wait_ge(*P("y", b))
                    dve.tensor_tensor(XB[:], pv[0:T, :], bo[:], ALU.add).then_inc(*V.done("y"))
                    dve.wait_ge(*V("y", b))
                    xb = G.X[:, bass.ds(b, 1), :].rearrange("p o d -> p (o d)")
                    dve.tensor_tensor(xb, xb, XB[:], ALU.add).then_inc(*V.done("yb"))

        @block.scalar
        def _(act):
            with mine(act):
                act.sem_inc(A.sem, len(A.names))
                act.wait_ge(s_w, 80)
                with act.Fori(0, B) as b:
                    act.wait_ge(*P(f"s{H1 - 1}", b - 1))
                    act.activation(QTb[:], G.QL[:, :, bass.ds(b * T, T)], ACT.Copy).then_inc(*A.done("q"))
                    act.wait_ge(*V(f"mv{KJ - 1}", b))
                    act.activation(rs[:, 0, :], mv[:, :, 1], ACT.Sqrt, bias=G.eps[:, 0:1]).then_inc(*A.done("std"))
                    for n, (k, g) in enumerate(turns):
                        lo, hi = g_of(g)
                        act.wait_ge(*P(f"x{k}{g}", b))
                        if n == 0:
                            act.wait_ge(*P(f"k{KD - 1}", b - 1))
                        act.activation(CT[:, k, lo * 128:hi * 128], pa[:, turns.index((k, g)) % 2, 0:(hi - lo) * 128], ACT.Identity,
                                       scale=gx[:, 0, k:k + 1], bias=gx[:, 1, k:k + 1]).then_inc(*A.done(f"x{k}{g}"))
                    for j in range(KJ):
                        act.wait_ge(*P(f"v{j}", b))
                        if j == 0:
                            act.wait_ge(*P(f"o{H1 - 1}", b - 1))
                        act.activation(Vv[:, j, :], pb[:, j % 2, :], ACT.Copy).then_inc(*A.done(f"v{j}"))
                    for p in range(KD):
                        act.wait_ge(*P(f"k{p}", b))
                        act.activation(pieces(KS[:]), pa[:, 0:NP, 0:PJ], ACT.Square).then_inc(*A.done(f"sq{p}"))
                        act.wait_ge(*V(f"fl{p}", b))
                        act.activation(NM[:], NM[:], ACT.Sqrt).then_inc(*A.done(f"nm{p}"))
                    for h in heads:
                        act.wait_ge(*V(f"n{h}", b))
                        if h >= 2:
                            act.wait_ge(*P(f"t{h - 2}", b))
                        act.activation(Pr[:, h % 2, :], S[:, h % 2, :], ACT.Exp, bias=nmx[:, h:h + 1],
                                       accum_out=Zs[:, h:h + 1]).then_inc(*A.done(f"e{h}"))
                        act.wait_ge(*P(f"t{h}", b))
                        if h >= 2:
                            act.wait_ge(*P(f"o{h - 2}", b))
                        pt = PT[:, h % 2]
                        act.activation(pt[:, 0:whole, :], pa[:, 0, 0:whole * T].rearrange("p (k t) -> p k t", t=T),
                                       ACT.Copy).then_inc(*A.done(f"ta{h}"))
                        if whole < KJ:
                            i, s = at(KJ - 1)
                            act.activation(pt[0:JTAIL, KJ - 1, :], pa[0:JTAIL, i, s], ACT.Copy).then_inc(*A.done(f"tb{h}"))
                        i, s = at(KJ)
                        act.activation(pt[0:T, KJ, :], pa[0:T, i, s], ACT.Copy).then_inc(*A.done(f"tc{h}"))
                    act.wait_ge(*P("ot", b))
                    act.activation(OT[:], pb[:, 0, 0:KD * T].rearrange("p (k t) -> p k t", t=T), ACT.Copy).then_inc(*A.done("ot"))

        @block.tensor
        def _(pe):
            pe.sem_inc(P.sem, len(P.names))
            pe.wait_ge(s_w, 80)

            def scores(h, b):
                r = slice(64 * (h % 2), 64 * (h % 2) + 64)
                if h == 0:
                    pe.wait_ge(*V(f"kt{KD - 1}", b))
                    pe.wait_ge(*GP("kl", b))
                    pe.wait_ge(*A("q", b))
                elif h >= 3 - NP:
                    pe.wait_ge(*V(f"s{h - 3 + NP}", b))
                for i in range(NP):
                    ins = pe.matmul(score_bank(h)[:, i, :], QTb[r, h // 2, :], KT[r, h // 2, i * HJ:(i + 1) * HJ],
                                    start=True, stop=True, tile_position=(64 * (h % 2), 0))
                ins.then_inc(*P.done(f"s{h}"))

            with mine(pe):
                with pe.Fori(0, B) as b:
                    pe.wait_ge(*V(f"c{KJ - 1}", b))
                    for n, (k, g) in enumerate(turns):
                        lo, hi = g_of(g)
                        pe.wait_ge(*(A(f"tc{H1 - 1}", b - 1) if n < 2 else A(f"x{turns[n - 2][0]}{turns[n - 2][1]}", b)))
                        for j in range(lo, hi):
                            ins = pe.transpose(pa[:, n % 2, (j - lo) * 128:(j - lo + 1) * 128], CN[:, j, k * 128:(k + 1) * 128],
                                               G.ident[:])
                        ins.then_inc(*P.done(f"x{k}{g}"))
                    pe.wait_ge(*A(f"x{KC - 1}{NG - 1}", b))
                    for j in range(KJ):
                        pe.wait_ge(*(A("ot", b - 1) if j < 2 else A(f"v{j - 2}", b)))
                        for k in range(KC):
                            ins = pe.matmul(pb[:, j % 2, :], CT[:, k, j * 128:(j + 1) * 128], Wkv[:, k, D:2 * D],
                                            start=k == 0, stop=k == KC - 1)
                        ins.then_inc(*P.done(f"v{j}"))
                    for p in range(KD):
                        if p:
                            pe.wait_ge(*V(f"kt{p - 1}", b))
                        for i in range(NP):
                            for k in range(KC):
                                ins = pe.matmul(pa[:, i, 0:PJ], Wkv[:, k, p * 128:(p + 1) * 128],
                                                CT[:, k, i * PJ:(i + 1) * PJ], start=k == 0, stop=k == KC - 1)
                        ins.then_inc(*P.done(f"k{p}"))
                        pe.wait_ge(*A(f"sq{p}", b))
                        if p == 0:
                            pe.wait_ge(*A(f"v{KJ - 1}", b))
                        for i in range(NP):
                            ins = pe.matmul(pb[:, i, 0:PJ], pair[:], KS[:, i * PJ:(i + 1) * PJ], start=True, stop=True)
                        ins.then_inc(*P.done(f"ss{p}"))
                    scores(0, b)
                    for h in heads:
                        if h + 1 < H1:
                            scores(h + 1, b)
                        pe.wait_ge(*A(f"e{h}", b))
                        if h:
                            pe.wait_ge(*A(f"tc{h - 1}", b))
                        for j, (o, n) in enumerate(tiles):
                            i, s = at(j)
                            ins = pe.transpose(pa[0:n, i, s], Pr[:, h % 2, o:o + n], G.ident[0:T, 0:T])
                        ins.then_inc(*P.done(f"t{h}"))
                        pe.wait_ge(*A(f"tc{h}", b))
                        if h == 0:
                            pe.wait_ge(*GP("vl", b))
                            pe.wait_ge(*V("o", b - 1))
                        for j, (o, n) in enumerate(tiles):
                            ins = pe.matmul(po[0:T, h * DH1:(h + 1) * DH1], PT[0:n, h % 2, j, :],
                                            Vv[0:n, j, h * DH1:(h + 1) * DH1], start=j == 0, stop=j == KJ)
                        ins.then_inc(*P.done(f"o{h}"))
                    pe.wait_ge(*V("o", b))
                    for k in range(KD):
                        ins = pe.transpose(pb[:, 0, k * T:(k + 1) * T], O[:, k * 128:(k + 1) * 128], G.ident[0:T, 0:T])
                    ins.then_inc(*P.done("ot"))
                    pe.wait_ge(*A("ot", b))
                    pe.wait_ge(*V("y", b - 1))
                    for k in range(KD):
                        ins = pe.matmul(pv[0:T, :], OT[:, k, :], Wo[:, k, :], start=k == 0, stop=k == KD - 1)
                    ins.then_inc(*P.done("y"))


def stage_store(nc, out, G):
    with ExitStack() as ctx:
        c = Core(nc, ctx, "store")
        s_out = c.sem("x_out")
        block = c.block()

        @block.sync
        def _(sp):
            sp.dma_start(out.rearrange("b t d -> t b d"), G.X[:]).then_inc(s_out, 16)
            sp.wait_ge(s_out, 16)


class Shared:
    pass


def build(nc, I, out, upto=99):
    with ExitStack() as ctx:
        c = Core(nc, ctx, "g")
        G = Shared()
        G.X, G.N, G.Y = c.sb("X", [T, B, D]), c.sb("N", [T, B, D]), c.sb("Y", [T, B, D])
        G.XT = c.sb("XT", [128, KD, NTOK])
        G.ident, G.eps = c.sb("ident", [128, 128]), c.sb("eps", [128, 1])
        G.slot, G.wt = c.sb("slot", [T, 2, B], I32), c.sb("wt", [T, 2, B])
        G.far, G.level = c.sb("far", [1, 1], I32), c.sb("level", [1, E], I32)
        G.xe0 = nc.dram_tensor("rows0", (E * CAP0 + NTOK, D), F32, kind="Internal").ap()
        G.ye0 = nc.dram_tensor("results0", (E * CAP0, D), F32, kind="Internal").ap()
        G.xe1 = nc.dram_tensor("rows1", (E * CAP1 + 2 * NTOK, D), F32, kind="Internal").ap()
        G.ye1 = nc.dram_tensor("results1", (E * CAP1, D), F32, kind="Internal").ap()
        with ExitStack() as part:
            p = Core(nc, part, "g0")
            G.Kf = p.sb("Kf", [NFREQ, 2, D])
            G.cpT = p.sb("cpT", [128, KC, NTOK])
            stage_s4d_kernel(nc, I, G)
            if upto >= 1:
                stage_topk_attention(nc, I, G)
                stage_film_conv(nc, I, G)
        if upto >= 1:
            stage_mlp(nc, I, G)
        if upto >= 2:
            with ExitStack() as part:
                first = FirstWeights(Core(nc, part, "experts1"))
                stage_router(nc, I, G, 1, I["gate_wT"], I["gate_b"], CAP0, G.xe0, first, I["e0_w1"], I["e0_w2"])
                stage_experts(nc, I, G, 1, ACT.Relu, I["e0_w1"], I["e0_b1"], I["e0_w2"], I["e0_b2"], CAP0, G.xe0, G.ye0,
                              first, (CAP0,))
        if upto >= 3:
            with ExitStack() as part:
                p = Core(nc, part, "g1")
                G.QL, G.KL = p.sb("QL", [128, KD, NTOK]), p.sb("KL", [128, KD, NTOK])
                G.VL = p.sb("VL", [T, B, D])
                stage_latents(nc, I, G)
                stage_attention(nc, I, G, "near", J - JNEAR, True)
                stage_attention(nc, I, G, "attn", 0, False)
        if upto >= 4:
            with ExitStack() as part:
                first = FirstWeights(Core(nc, part, "experts2"))
                stage_router(nc, I, G, 2, I["Wg"], I["zero8"], CAP1, G.xe1, first, I["e1_w1"], I["e1_w2"])
                stage_experts(nc, I, G, 2, ACT.Gelu, I["e1_w1"], I["e1_b1"], I["e1_w2"], I["e1_b2"], CAP1, G.xe1, G.ye1,
                              first, WIDTHS)
        stage_store(nc, out, G)


def constants():
    l, f = np.arange(T), np.arange(NFREQ)
    ang = np.pi * np.outer(l, f) / T
    weight = np.where((f == 0) | (f == T), 1.0, 2.0)[:, None] / (2 * T)
    fold = np.zeros((4, 32, LB, 2, NFREQ))
    for a in range(LA):
        for b in range(LB):
            fold[:, a, b, 0, :] = np.cos(ang[LB * a + b])
            fold[:, a, b, 1, :] = np.sin(ang[LB * a + b])
    t = np.arange(NTOK).reshape(B, T).T
    return {
        "ident": np.eye(128), "dft_fold": fold.reshape(128, LB, 2, NFREQ),
        "Fc": np.cos(ang), "Fs": np.sin(ang),
        "Gc": weight * np.cos(ang).T, "Gn": -weight * np.cos(ang).T, "Gs": weight * np.sin(ang).T,
        "iota_m8": np.arange(E) - 8.0, "tri": np.triu(np.ones((T, T))), "ones": np.ones((T, T)),
        "trash1": np.stack([E * CAP0 + t, E * CAP0 + t], 1),
        "trash2": np.stack([E * CAP1 + t, E * CAP1 + NTOK + t], 1),
        "pair": np.kron(np.eye(2), np.ones((DH1, DH1))), "zero8": np.zeros(E),
    }


def layout(x):
    c = np.ascontiguousarray
    by_p = lambda v: c(v.reshape(E, KF, 128).transpose(2, 0, 1))
    u8 = lambda m: c(m)
    L0, L1 = "L0_xattn_", "L1_xattn_"
    a = {
        "x": x["x"], "ctx": x["ctx_768"], "ctxT": x["ctx_768"].transpose(0, 2, 1),
        "log_dt": x[L0 + "log_dt"].reshape(D // 128, 128).T, "A_re": x[L0 + "A_re"], "A_im": x[L0 + "A_im"], "C_re": x[L0 + "C_re"],
        "C_im": x[L0 + "C_im"], "D_skip": x[L0 + "D_skip"], "mod_gate": x[L0 + "mod_gate"].reshape(1),
        "tmask": u8(x["mask_BxS_bf1"].T), "vmask": u8(x["mask_BxS2_bf1"]), "kmask": u8(x["mask_BxS2_bk0"]),
        "L0_Wq": x[L0 + "Wq"], "L0_Wk": x[L0 + "Wk"], "L0_Wv": x[L0 + "Wv"],
        "Wf_in": x[L0 + "W_film_in"], "bf_in": x[L0 + "b_film_in"],
        "Wf_out": x[L0 + "W_film_out"], "bf_out": x[L0 + "b_film_out"],
        "g_in": x[L0 + "g_norm_in"], "b_in": x[L0 + "b_norm_in"], "g_ffn": x[L0 + "g_ffn"], "b_ffn": x[L0 + "b_ffn"],
        "g_out": x[L0 + "g_norm_out"], "b_out": x[L0 + "b_norm_out"],
        "W1": x[L0 + "W1"], "b1": x[L0 + "b1"].reshape(KF, 128).T, "W2": x[L0 + "W2"], "b2": x[L0 + "b2"],
        "gate_wT": x["L0_ffn_gate_w"].T, "gate_b": x["L0_ffn_gate_b"],
        "e0_w1": x["L0_ffn_w1"], "e0_b1": by_p(x["L0_ffn_b1"]), "e0_w2": x["L0_ffn_w2"], "e0_b2": x["L0_ffn_b2"],
        "ln_x": np.stack([x[L1 + "ln_x_g"].reshape(KC, 128).T, x[L1 + "ln_x_b"].reshape(KC, 128).T], 1),
        "ln_l_g": x[L1 + "ln_l_g"], "ln_l_b": x[L1 + "ln_l_b"], "qn_g": x[L1 + "qn_g"].reshape(DH1, 1), "kn_g": x[L1 + "kn_g"].reshape(DH1, 1),
        "WqT": x[L1 + "Wq"].T, "WkvT": x[L1 + "Wkv"].T, "WlkvT": x[L1 + "Wlkv"].T, "WoT": x[L1 + "Wo"].T,
        "bo": x[L1 + "bo"],
        "Wg": x["L1_ffn_Wg"], "e1_w1": x["L1_ffn_W1"], "e1_b1": by_p(x["L1_ffn_b1"]), "e1_w2": x["L1_ffn_W2"],
        "e1_b2": x["L1_ffn_b2"],
    }
    a = {n: c(v) for n, v in a.items()}
    a.update({n: c(v.astype(np.float32)) for n, v in constants().items()})
    return a


UPTO = 99


def kernel(**inputs):
    import concourse.bacc as _bacc
    from concourse.bass_utils import run_bass_kernel_spmd as _run

    nc = _bacc.Bacc("TRN2", target_bir_lowering=False, num_devices=1)
    arrays, I = {}, {}
    for name, a in layout({n: np.asarray(v) for n, v in inputs.items()}).items():
        arrays[f"in_{name}_dram"] = a
        I[name] = nc.dram_tensor(f"in_{name}_dram", a.shape, mybir.dt.from_np(a.dtype), kind="ExternalInput").ap()
    out = nc.dram_tensor("out_0_dram", (B, T, D), F32, kind="ExternalOutput").ap()
    build(nc, I, out, UPTO)
    r = _run(nc, [arrays], core_ids=[0])
    return r.results[0]["out_0_dram"]
```
